# Optimizing a Trainium2 kernel written in Bass

```python
import numpy as np
import jax
import jax.numpy as jnp

def _softmax(x, axis=-1):
    return jax.nn.softmax(x, axis=axis)

def _gelu(x):
    return jax.nn.gelu(x, approximate=True)

def _silu(x):
    return jax.nn.silu(x)

def _sigmoid(x):
    return jax.nn.sigmoid(x)

def _layernorm(x, axis=-1, eps=1e-05):
    m = jnp.mean(x, axis=axis, keepdims=True)
    v = jnp.var(x, axis=axis, keepdims=True)
    return (x - m) / jnp.sqrt(v + eps)

def _scatter_add(tgt, idx, src, axis=0):
    return tgt.at[idx].add(src)

def _segment_sum(src, seg, n):
    return jax.ops.segment_sum(src, seg, n)
kernel_name = 'mk_decoder_postln_d1_seqx_r4_080300'

def setup_inputs(seed: int=0):
    np.random.seed(seed)
    _w = jnp.asarray

    def _rec_inputs():
        import jax
        import jax.numpy as jnp
        _rk = jax.random.key(seed)
        x = -0.0002928 + 1 * jax.random.normal(jax.random.fold_in(_rk, 1), (2, 1024, 256), jnp.float32)
        _lenS = 1024 - jax.random.randint(jax.random.fold_in(_rk, 7), (2,), 0, max(1, 1024 // 4) + 1, jnp.int32)
        _lenS2 = 77 - jax.random.randint(jax.random.fold_in(_rk, 8), (2,), 0, max(1, 77 // 4) + 1, jnp.int32)
        _ctx_1024P = jax.random.normal(jax.random.fold_in(_rk, 11), (2, 16, 256), jnp.float32)
        _ctx_1024c = jax.random.dirichlet(jax.random.fold_in(_rk, 511), 0.3 * jnp.ones((16,), jnp.float32), (2, 77))
        _ctx_1024t = jnp.einsum('bsk,bkd->bsd', _ctx_1024c, _ctx_1024P)
        _ctx_1024t = _ctx_1024t * jax.lax.rsqrt(jnp.mean(jnp.square(_ctx_1024t)) + 1e-12) * 0.953939
        ctx_1024 = -1.39393e-06 + 0.999914 * (_ctx_1024t + 0.3 * jax.random.normal(jax.random.fold_in(_rk, 611), (2, 77, 256), jnp.float32))
        _validS = jnp.arange(1024)[None, :] < _lenS[:, None]
        _validS2 = jnp.arange(77)[None, :] < _lenS2[:, None]
        _causal = jnp.tril(jnp.ones((1024, 1024), dtype=bool))
        mask_1x1xSxS2_bk1 = jnp.broadcast_to(_validS2[0:1, None, None, :], (1, 1, 1024, 77))
        return (x, ctx_1024, mask_1x1xSxS2_bk1)
    x, ctx_1024, mask_1x1xSxS2_bk1 = _rec_inputs()

    def _L0_attn_setup():
        import jax, jax.numpy as jnp
        import numpy as np
        D = 256
        B = 4
        S = 1024
        LN_EPS = 1e-05

        def _layer_norm(x, gamma, beta):
            mu = jnp.mean(x, axis=-1, keepdims=True)
            var = jnp.mean(jnp.square(x - mu), axis=-1, keepdims=True)
            return (x - mu) * jax.lax.rsqrt(var + LN_EPS) * gamma + beta
        key = jax.random.key(seed)
        ks = jax.random.split(key, 5)
        scale = 1.0 / np.sqrt(D)
        return {'hidden_states': jax.random.normal(ks[0], (B, S, D), dtype=jnp.float32), 'attention_mask': jnp.ones((B, S), dtype=jnp.int32), 'Wk': jax.random.normal(ks[1], (D, D), dtype=jnp.float32) * scale, 'bk': jnp.zeros((D,), dtype=jnp.float32), 'Wka': jax.random.normal(ks[2], (D, D), dtype=jnp.float32) * scale, 'bka': jnp.zeros((D,), dtype=jnp.float32), 'Wv': jax.random.normal(ks[3], (D, D), dtype=jnp.float32) * scale, 'bv': jnp.zeros((D,), dtype=jnp.float32), 'gamma': jnp.ones((D,), dtype=jnp.float32), 'beta': jnp.zeros((D,), dtype=jnp.float32)}
    _L0_attn_all = _L0_attn_setup()
    _L0_attn_in = {k: v for k, v in _L0_attn_all.items() if k in ('attention_mask', 'Wk', 'bk', 'Wka', 'bka', 'Wv', 'bv', 'gamma', 'beta')}
    del _L0_attn_all

    def _L0_xattn_setup():
        import jax, jax.numpy as jnp
        import numpy as np
        D_MODEL = 256
        NUM_HEADS = 16
        D_K = D_MODEL // NUM_HEADS

        def _split(x):
            B, S, _ = x.shape
            return x.reshape(B, S, NUM_HEADS, D_K).transpose(0, 2, 1, 3)
        key = jax.random.key(seed)
        ks = jax.random.split(key, 8)
        B, S = (2, 512)
        query = jax.random.normal(ks[0], (B, S, D_MODEL), dtype=jnp.float32)
        k_in = jax.random.normal(ks[1], (B, S, D_MODEL), dtype=jnp.float32)
        value = jax.random.normal(ks[2], (B, S, D_MODEL), dtype=jnp.float32)
        mask = jnp.triu(jnp.ones((S, S), dtype=bool), k=1)[None, None, :, :]
        scale = 1.0 / np.sqrt(D_MODEL)
        W_q = jax.random.normal(ks[3], (D_MODEL, D_MODEL), dtype=jnp.float32) * scale
        W_k = jax.random.normal(ks[4], (D_MODEL, D_MODEL), dtype=jnp.float32) * scale
        W_v = jax.random.normal(ks[5], (D_MODEL, D_MODEL), dtype=jnp.float32) * scale
        W_o = jax.random.normal(ks[6], (D_MODEL, D_MODEL), dtype=jnp.float32) * scale
        return {'query': query, 'key': k_in, 'value': value, 'mask': mask, 'W_q': W_q, 'W_k': W_k, 'W_v': W_v, 'W_o': W_o}
    _L0_xattn_all = _L0_xattn_setup()
    _L0_xattn_in = {k: v for k, v in _L0_xattn_all.items() if k in ('W_q', 'W_k', 'W_v', 'W_o')}
    del _L0_xattn_all

    def _L0_ffn_setup():
        import jax, jax.numpy as jnp
        import numpy as np
        B, S, H = (8, 256, 256)
        FF = 1024
        E = 8
        TOP_K = 2
        LN_EPS = 1e-12

        def _layernorm(x, w, b):
            mu = jnp.mean(x, axis=-1, keepdims=True)
            var = jnp.mean(jnp.square(x - mu), axis=-1, keepdims=True)
            return (x - mu) * jax.lax.rsqrt(var + LN_EPS) * w + b
        key = jax.random.key(seed)
        ks = jax.random.split(key, 8)
        sc_h = 1.0 / np.sqrt(H)
        sc_ff = 1.0 / np.sqrt(FF)
        return {'hidden_states': jax.random.normal(ks[0], (B, S, H), jnp.float32), 'router_w': jax.random.normal(ks[1], (E, H), jnp.float32) * sc_h, 'router_b': jnp.zeros((E,), jnp.float32), 'w1': jax.random.normal(ks[2], (E, FF, H), jnp.float32) * sc_h, 'b1': jax.random.normal(ks[3], (E, FF), jnp.float32) * 0.01, 'w2': jax.random.normal(ks[4], (E, H, FF), jnp.float32) * sc_ff, 'b2': jax.random.normal(ks[5], (E, H), jnp.float32) * 0.01, 'ln_w': jnp.ones((H,), jnp.float32), 'ln_b': jnp.zeros((H,), jnp.float32)}
    _L0_ffn_all = _L0_ffn_setup()
    _L0_ffn_in = {k: v for k, v in _L0_ffn_all.items() if k in ('router_w', 'router_b', 'w1', 'b1', 'w2', 'b2', 'ln_w', 'ln_b')}
    del _L0_ffn_all
    return {'x': x, 'ctx_1024': ctx_1024, 'mask_1x1xSxS2_bk1': mask_1x1xSxS2_bk1, 'L0_attn_attention_mask': _L0_attn_in['attention_mask'], 'L0_attn_Wk': _L0_attn_in['Wk'], 'L0_attn_bk': _L0_attn_in['bk'], 'L0_attn_Wka': _L0_attn_in['Wka'], 'L0_attn_bka': _L0_attn_in['bka'], 'L0_attn_Wv': _L0_attn_in['Wv'], 'L0_attn_bv': _L0_attn_in['bv'], 'L0_attn_gamma': _L0_attn_in['gamma'], 'L0_attn_beta': _L0_attn_in['beta'], 'L0_xattn_W_q': _L0_xattn_in['W_q'], 'L0_xattn_W_k': _L0_xattn_in['W_k'], 'L0_xattn_W_v': _L0_xattn_in['W_v'], 'L0_xattn_W_o': _L0_xattn_in['W_o'], 'L0_ffn_router_w': _L0_ffn_in['router_w'], 'L0_ffn_router_b': _L0_ffn_in['router_b'], 'L0_ffn_w1': _L0_ffn_in['w1'], 'L0_ffn_b1': _L0_ffn_in['b1'], 'L0_ffn_w2': _L0_ffn_in['w2'], 'L0_ffn_b2': _L0_ffn_in['b2'], 'L0_ffn_ln_w': _L0_ffn_in['ln_w'], 'L0_ffn_ln_b': _L0_ffn_in['ln_b']}

def reference(x, ctx_1024, mask_1x1xSxS2_bk1, L0_attn_attention_mask, L0_attn_Wk, L0_attn_bk, L0_attn_Wka, L0_attn_bka, L0_attn_Wv, L0_attn_bv, L0_attn_gamma, L0_attn_beta, L0_xattn_W_q, L0_xattn_W_k, L0_xattn_W_v, L0_xattn_W_o, L0_ffn_router_w, L0_ffn_router_b, L0_ffn_w1, L0_ffn_b1, L0_ffn_w2, L0_ffn_b2, L0_ffn_ln_w, L0_ffn_ln_b):
    import jax
    import jax.numpy as jnp

    def _L0_attn_ref(hidden_states, attention_mask, Wk, bk, Wka, bka, Wv, bv, gamma, beta):
        import jax, jax.numpy as jnp
        import numpy as np
        D = 256
        B = 4
        S = 1024
        LN_EPS = 1e-05

        def _layer_norm(x, gamma, beta):
            mu = jnp.mean(x, axis=-1, keepdims=True)
            var = jnp.mean(jnp.square(x - mu), axis=-1, keepdims=True)
            return (x - mu) * jax.lax.rsqrt(var + LN_EPS) * gamma + beta
        h = _layer_norm(hidden_states, gamma, beta)
        d_model = h.shape[-1]
        keys = jnp.einsum('bsd,ed->bse', h, Wk) + bk
        values = jnp.einsum('bsd,ed->bse', h, Wv) + bv
        key_att = jnp.einsum('bsd,ed->bse', keys, Wka) + bka
        keys_weight = jnp.exp(key_att / jnp.sqrt(jnp.asarray(d_model, h.dtype)))
        keys_weight = keys_weight / jnp.cumsum(keys_weight, axis=1)
        pooled_keys = jnp.cumsum(keys_weight * keys, axis=1)
        return pooled_keys * values

    def _L0_xattn_ref(query, key, value, mask, W_q, W_k, W_v, W_o):
        import jax, jax.numpy as jnp
        import numpy as np
        D_MODEL = 256
        NUM_HEADS = 16
        D_K = D_MODEL // NUM_HEADS

        def _split(x):
            B, S, _ = x.shape
            return x.reshape(B, S, NUM_HEADS, D_K).transpose(0, 2, 1, 3)
        Q = _split(query @ W_q.T)
        K = _split(key @ W_k.T)
        V = _split(value @ W_v.T)
        scores = jnp.einsum('bhqd,bhkd->bhqk', Q, K) / jnp.sqrt(jnp.float32(D_K))
        scores = jnp.where(mask, -jnp.inf, scores)
        attn_w = jax.nn.softmax(scores, axis=-1)
        attn_w = jnp.nan_to_num(attn_w, nan=0.0)
        out = jnp.einsum('bhqk,bhkd->bhqd', attn_w, V)
        B, _, Sq, _ = out.shape
        merged = out.transpose(0, 2, 1, 3).reshape(B, Sq, D_MODEL)
        return merged @ W_o.T

    def _L0_ffn_ref(hidden_states, router_w, router_b, w1, b1, w2, b2, ln_w, ln_b):
        import jax, jax.numpy as jnp
        import numpy as np
        B, S, H = (8, 256, 256)
        FF = 1024
        E = 8
        TOP_K = 2
        LN_EPS = 1e-12

        def _layernorm(x, w, b):
            mu = jnp.mean(x, axis=-1, keepdims=True)
            var = jnp.mean(jnp.square(x - mu), axis=-1, keepdims=True)
            return (x - mu) * jax.lax.rsqrt(var + LN_EPS) * w + b
        b, s, h = hidden_states.shape
        flat = hidden_states.reshape(-1, h)
        logits = flat @ router_w.T + router_b
        topk_vals, topk_idx = jax.lax.top_k(logits, TOP_K)
        topk_w = jax.nn.softmax(topk_vals, axis=-1)
        out = jnp.zeros_like(flat)
        n_exp = w1.shape[0]
        for e in range(n_exp):
            cw = jnp.sum(jnp.where(topk_idx == e, topk_w, 0.0), axis=-1)
            y = jax.nn.gelu(flat @ w1[e].T + b1[e], approximate=False)
            y = y @ w2[e].T + b2[e]
            out = out + y * cw[:, None]
        out = out.reshape(b, s, h) + hidden_states
        return _layernorm(out, ln_w, ln_b)
    x = _layernorm(x + _L0_attn_ref(x, L0_attn_attention_mask, L0_attn_Wk, L0_attn_bk, L0_attn_Wka, L0_attn_bka, L0_attn_Wv, L0_attn_bv, L0_attn_gamma, L0_attn_beta), axis=-1)
    x = _layernorm(x + _L0_xattn_ref(x, ctx_1024, ctx_1024, mask_1x1xSxS2_bk1, L0_xattn_W_q, L0_xattn_W_k, L0_xattn_W_v, L0_xattn_W_o), axis=-1)
    x = _layernorm(x + _L0_ffn_ref(x, L0_ffn_router_w, L0_ffn_router_b, L0_ffn_w1, L0_ffn_b1, L0_ffn_w2, L0_ffn_b2, L0_ffn_ln_w, L0_ffn_ln_b), axis=-1)
    return x

_drawn_inputs = setup_inputs


def setup_inputs(seed=0):
    import zlib

    import numpy as np

    out = dict(_drawn_inputs(seed))
    spreads = {'L0_attn_bk': (0.0, 0.1),
     'L0_attn_bka': (0.0, 2.0),
     'L0_attn_bv': (0.0, 0.1),
     'L0_attn_gamma': (1.0, 0.2),
     'L0_attn_beta': (0.0, 0.1),
     'L0_ffn_router_b': (0.0, 0.1),
     'L0_ffn_ln_w': (1.0, 0.2),
     'L0_ffn_ln_b': (0.0, 0.1)}
    factors = {'L0_ffn_b1': 23.703, 'L0_ffn_b2': 8.0}
    for name, (base, spread) in spreads.items():
        noise = np.random.default_rng([zlib.crc32(name.encode()), seed]).standard_normal(out[name].shape)
        drawn = base * np.exp(spread * noise) if base else spread * noise
        out[name] = jnp.asarray(drawn.astype(out[name].dtype))
    for name, factor in factors.items():
        out[name] = (out[name] * factor).astype(out[name].dtype)
    return out
```

```python
from contextlib import ExitStack

import concourse.bass as bass
from concourse import mybir

F32 = mybir.dt.float32
BF16 = mybir.dt.bfloat16
I32 = mybir.dt.int32
U32 = mybir.dt.uint32
U8 = mybir.dt.uint8
ALU = mybir.AluOpType
ACT = mybir.ActivationFunctionType
AX = mybir.AxisListType

P = 128
B, S, D = 2, 1024, 256
T = B * S
KD = D // P
TILES = T // P
CT = 4
CHUNK = CT * P
CPB = S // CHUNK
CHUNKS = T // CHUNK
SC = 77
HEADS, DK = 16, 16
HC = P // DK
HG = 4
VW = DK + 1
E, FF = 8, 1024
KF = FF // P
TOPK = 2
SLOT_TILES = TOPK * T // P + E - 1
XS_TILES = SLOT_TILES + 1
EPS = 1e-5
EPS_FFN = 1e-12
MASKED = -1e30
UNITS = CT * KD


def decoder_layer(nc, x, ctxT, maskT, wk, bk, wka, bka, wv, bv, gamma, beta, wq, wxk, wxv, wo,
                  rw, rb, w1, b1, w2, b2, lnw, lnb, out):
    xs = nc.dram_tensor("sorted_tokens", [XS_TILES * P, D], F32).ap()
    ys = nc.dram_tensor("sorted_outputs", [SLOT_TILES * P, D], F32).ap()

    x_rows = x.rearrange("(t p) d -> p t d", p=P)
    out_rows = out.rearrange("(t p) d -> p t d", p=P)
    xs_tiles = xs.rearrange("(t p) d -> p t d", p=P)
    ys_tiles = ys.rearrange("(t p) d -> p t d", p=P)

    with ExitStack() as ctx:
        def sb(name, shape, dt=F32):
            return ctx.enter_context(nc.sbuf_tensor(name, shape, dt))

        def sem(name):
            return ctx.enter_context(nc.semaphore(name))

        W1 = sb("expert_w1", [P, E * KD * FF])
        W2 = sb("expert_w2", [P, E * KF * D])
        LATE = sb("front_weights_then_b1", [P, E * FF])
        X2 = sb("x2", [P, TILES, D])
        R = sb("work", [P, 5888])
        w1_v = W1[:, :].rearrange("p (e k f) -> p e k f", e=E, k=KD)
        w2_v = W2[:, :].rearrange("p (e k n) -> p e k n", e=E, k=KF)
        EW = KD * FF
        EARLY = 5

        def slot(n):
            t, m = (W1, n) if n < 6 else (W2, n - 6)
            return t[:, EARLY * EW + m * 1024:EARLY * EW + (m + 1) * 1024]

        def by_tile(ap):
            return ap.rearrange("p (j d) -> p j d", j=CT)

        def by_chunk(ap):
            return ap.rearrange("p (k n) -> p k n", k=KD)

        xc = by_tile(slot(0))
        h0 = by_tile(slot(1))
        hT = by_chunk(slot(2))
        keysT = by_chunk(slot(3))
        kexp = by_chunk(slot(4))
        csum = by_chunk(slot(5))
        kw = by_chunk(slot(6))
        pooled = by_chunk(slot(7))
        attnT = by_chunk(slot(8))
        x1 = by_tile(slot(9))
        x1T = by_chunk(slot(10))
        qT = by_chunk(slot(11))
        x2c = by_tile(slot(6))
        x2T = by_chunk(slot(3))

        off = [0]

        def late(n):
            off[0] += n
            return LATE[:, off[0] - n:off[0]]

        def late_w():
            return late(KD * D).rearrange("p (k n) -> p k n", k=KD)

        wk_s, wka_s, wv_s, wq_s, wo_s, wxk_s, wxv_s = (late_w() for _ in range(7))
        kbd = late(B * HEADS * SC).rearrange("p (b c h k) -> p b c h k", b=B, c=KD, h=HC)
        vaug = late(B * HEADS * VW).rearrange("p (b h v) -> p b h v", b=B, h=HEADS)
        ctx_s = late(KD * B * SC).rearrange("p (k n) -> p k n", k=KD)
        rw_s = late(KD * E).rearrange("p (k e) -> p k e", k=KD)
        rb_s = late(E)
        assert off[0] <= E * FF
        b1_s = LATE[:, :].rearrange("p (e f) -> p e f", e=E)

        prob = R[:, 0:1232].rearrange("p (s h k) -> p s h k", s=2, h=HC)
        probT = R[:, 1232:3280].rearrange("p (s h q) -> p s h q", s=2, h=HC)
        merged = R[:, 3280:3792].rearrange("p (s d) -> p s d", s=2)
        mergedT = R[:, 3792:4304].rearrange("p (s k q) -> p s k q", s=2, k=KD)
        xt = R[:, 0:256]
        xtT = R[:, 256:512].rearrange("p (k q) -> p k q", k=KD)
        hb = R[:, 512:1536]
        hg = R[:, 1536:2560]
        hgT = R[:, 2560:3584].rearrange("p (k q) -> p k q", k=KF)
        yt = R[:, 3584:3840]
        b2_s = R[:, 3840:5888].rearrange("p (e d) -> p e d", e=E)
        y_of = [W1[:, c * TILES * D:(c + 1) * TILES * D].rearrange("p (t d) -> p t d", t=TILES) for c in range(TOPK)]
        acc = W2[:, 0:1024].rearrange("p (j d) -> p j d", j=CT)
        zed = W2[:, 1024:2048].rearrange("p (j d) -> p j d", j=CT)
        fin = W2[:, 2048:6144].rearrange("p (t d) -> p t d", t=TILES)
        lnw_s = W2[:, 6144:6144 + D]
        lnb_s = W2[:, 6400:6400 + D]

        ident = sb("identity", [P, P])
        mask_b = sb("mask_bias", [P, S], BF16)
        mask_raw = slot(11)[0:SC, 0:S // 4].bitcast(U8)
        eye4 = sb("identity_per_head", [P, HG, SC], BF16)
        gam = sb("gamma", [P, KD])
        bet = sb("beta", [P, KD])
        bk_s = sb("bk", [P, KD])
        bka_s = sb("bka", [P, KD])
        bv_s = sb("bv", [P, KD])
        stats = sb("ln_stats", [P, CT, 6])
        mdiff, msum, vsum, msq, mean = (sb(f"ln_{n}", [P, CT]) for n in ("mdiff", "msum", "vsum", "msq", "mean"))
        veps = sb("ln_var_eps", [P, CT])
        rstd = sb("ln_rstd", [P, CT])
        mhalf = sb("minus_half", [P, CT])
        one_c = sb("one", [P, 1])
        smax = sb("score_max", [P, 2, HEADS])
        psum_r = sb("prob_sum_recip", [P, HEADS])
        pscale = sb("prob_scale", [P, HEADS])
        logits = sb("logits", [P, TILES, E])
        weight = [sb(f"choice_weight{c}", [P, TILES]) for c in range(TOPK)]
        where = [sb(f"choice_slot{c}", [P, TILES], U32) for c in range(TOPK)]
        expert_of = sb("expert_of_tile", [P, XS_TILES], I32)

        at = [0]

        def tmp(*shape):
            n = 1
            for m in shape:
                n *= m
            at[0] += n
            assert at[0] <= 3840
            v = R[:, at[0] - n:at[0]]
            if len(shape) == 2:
                v = v.rearrange("p (a b) -> p a b", a=shape[0])
            return v

        m1, m2, first = tmp(TILES), tmp(TILES), tmp(TILES)
        hot = [tmp(TILES, E) for _ in range(TOPK)]
        cand, rest = tmp(TILES, E), tmp(TILES, E)
        both = tmp(TILES, E)
        ex, den = tmp(TILES), tmp(TILES)
        tot, run = tmp(E, TILES), tmp(E, TILES)
        ones_r = tmp(E * TILES)
        starts, count, ntile, tbend, adj = tmp(E), tmp(E), tmp(E), tmp(E), tmp(E)
        counti = tmp(E)
        slots = tmp(TILES, E)
        picked = tmp(TILES, E)
        slotf = tmp(TILES)
        rev = tmp(E)
        tau = tmp(XS_TILES, E)
        tge = tmp(XS_TILES, E)
        tri = tmp(P)
        ones_m = tmp(P)
        tilef = tmp(XS_TILES)

        zero_t = X2[:, TILES - 1, :]
        hmask = slot(8)[:, 0:HC]

        pa = ctx.enter_context(nc.psum_tensor("psum_a", [P, KD, 512], F32))
        pb = ctx.enter_context(nc.psum_tensor("psum_b", [P, KD, 512], F32))
        pc = ctx.enter_context(nc.psum_tensor("psum_c", [P, KD, 512], F32))
        pv = ctx.enter_context(nc.psum_tensor("psum_v", [P, 512], F32))
        pm = ctx.enter_context(nc.psum_tensor("psum_m", [P, 512], F32))
        score = [pa, pb]
        pb_t = pb[:, :, :].rearrange("p a (b d) -> p (a b) d", d=D)

        (consts_in, weights_in, ctx_in, experts_in, late_in, ln_in, zero_made, pads_zeroed, made, mask_made,
         ctx_mm, kv_made, x_in, x_free, ln_stats, ln_mv, ln_var, ln_rstd, h0_ready, hT_mm, hT_ready, k_mm, kT_ready,
         ka_mm, kexp_ready, scanned, recip_ready, kw_part, kw_ready, pooled_ready, v_mm, attn_ready, at_mm, r1_ready,
         x1_ready, x1T_mm, x1T_ready, q_mm, qT_ready, s_mm, max_ready, sub_ready, exp_ready, pT_mm, pT_ready, pv_mm,
         rec_ready, scale_ready, merged_ready, mT_mm, mT_ready, o_mm, r2_ready, x2_ready, x2_kept, x2T_mm, x2T_ready,
         lg_mm, lg_ready, bka_ready, carry_reset) = (sem(n) for n in (
             "consts_in weights_in ctx_in experts_in late_in ln_in zero_made pads_zeroed made mask_made "
             "ctx_mm kv_made x_in x_free ln_stats_s ln_mv_s ln_var_s ln_rstd_s h0_ready hT_mm hT_ready k_mm kT_ready "
             "ka_mm kexp_ready scanned recip_ready kw_part kw_ready pooled_ready v_mm attn_ready at_mm r1_ready "
             "x1_ready x1T_mm x1T_ready q_mm qT_ready s_mm max_ready sub_ready exp_ready pT_mm pT_ready pv_mm "
             "rec_ready scale_ready merged_ready mT_mm mT_ready o_mm r2_ready x2_ready x2_kept x2T_mm x2T_ready "
             "lg_mm lg_ready bka_ready carry_reset").split())
        (route_consts, route, ex_ready, count_mm, slots_ready, scattered, table_ready, xt_in, xt_mm, xt_ready, h_mm,
         hb_ready, hg_ready, hgT_mm, hgT_ready, y_mm, y_ready, y_out, fin_step, f_var, f_rstd, fin_ready, fin_out,
         route_rows) = (
            sem(n) for n in (
                "route_consts route ex_ready count_mm slots_ready scattered table_ready xt_in xt_mm xt_ready h_mm "
                "hb_ready hg_ready hgT_mm hgT_ready y_mm y_ready y_out fin_step f_var f_rstd fin_ready fin_out "
                "route_rows").split())
        gathered = [sem(f"gathered{t}") for t in range(TILES)]

        block = ctx.enter_context(nc.Block())

        @block.sync
        def _(sp):
            sp.dma_start(xc, x_rows[:, 0:CT, :]).then_inc(x_in, 16)
            for dst, src in ((gam, gamma), (bet, beta), (bk_s, bk), (bka_s, bka), (bv_s, bv)):
                with nc.allow_non_contiguous_dma(reason="256 values, one per partition"):
                    sp.dma_start(dst[:, :], src.rearrange("(k p) -> p k", p=P)).then_inc(consts_in, 16)
            for dst, src in ((wk_s, wk), (wka_s, wka), (wv_s, wv)):
                sp.dma_start(dst, src.rearrange("(k p) n -> p k n", p=P)).then_inc(weights_in, 16)
            sp.dma_start(ctx_s, ctxT.rearrange("(k p) n -> p k n", p=P)).then_inc(ctx_in, 16)
            sp.dma_start(mask_raw, maskT).then_inc(ctx_in, 16)
            for dst, src in ((wxk_s, wxk), (wxv_s, wxv), (wq_s, wq), (wo_s, wo)):
                sp.dma_start(dst, src.rearrange("(k p) n -> p k n", p=P)).then_inc(ctx_in, 16)
            sp.dma_start(rw_s, rw.rearrange("(k p) e -> p k e", p=P)).then_inc(ctx_in, 16)
            sp.dma_start(rb_s, rb.partition_broadcast(P)).then_inc(ctx_in, 16)
            sp.wait_ge(zero_made, 1)
            sp.dma_start(xs_tiles, zero_t.rearrange("p (a d) -> p a d", a=1).to_broadcast([P, XS_TILES, D])).then_inc(pads_zeroed, 16)
            for e in range(EARLY):
                sp.dma_start(w1_v[:, e], w1[e].rearrange("(k p) f -> p k f", p=P)).then_inc(experts_in, 16)
                sp.dma_start(w2_v[:, e], w2[e].rearrange("(k p) d -> p k d", p=P)).then_inc(experts_in, 16)
            with sp.Fori(0, CHUNKS - 1) as it:
                sp.wait_ge(x_free, it + 1)
                sp.dma_start(xc, x_rows[:, bass.ds(it * CT + CT, CT), :]).then_inc(x_in, 16)
            sp.wait_ge(lg_ready, CHUNKS)
            sp.wait_ge(x2_kept, CHUNKS)
            for e in range(EARLY, E):
                sp.dma_start(w1_v[:, e], w1[e].rearrange("(k p) f -> p k f", p=P)).then_inc(experts_in, 16)
                sp.dma_start(w2_v[:, e], w2[e].rearrange("(k p) d -> p k d", p=P)).then_inc(experts_in, 16)
            sp.dma_start(LATE[:, :], b1.rearrange("e f -> (e f)").partition_broadcast(P)).then_inc(late_in, 16)
            sp.dma_start(R[:, 3840:5888], b2.rearrange("e d -> (e d)").partition_broadcast(P)).then_inc(late_in, 16)

            sp.wait_ge(scattered, TOPK * TILES * 16)
            sp.wait_ge(route, ROUTE_STEPS)
            sp.dma_start(xt, xs_tiles[:, 0, :]).then_inc(xt_in, 16)
            sp.wait_ge(xt_mm, 1)
            sp.dma_start(xt, xs_tiles[:, 1, :]).then_inc(xt_in, 16)
            with sp.Fori(1, SLOT_TILES) as t:
                sp.wait_ge(xt_mm, t + 1)
                sp.dma_start(xt, xs_tiles[:, bass.ds(t + 1, 1), :]).then_inc(xt_in, 16)
                sp.wait_ge(y_ready, t)
                sp.dma_start(ys_tiles[:, bass.ds(t - 1, 1), :], yt).then_inc(y_out, 16)
            sp.wait_ge(y_ready, SLOT_TILES)
            sp.dma_start(ys_tiles[:, SLOT_TILES - 1, :], yt).then_inc(y_out, 16)
            sp.dma_start(lnw_s, lnw.partition_broadcast(P)).then_inc(ln_in, 16)
            sp.dma_start(lnb_s, lnb.partition_broadcast(P)).then_inc(ln_in, 16)
            for g in range(TILES // CT):
                sp.wait_ge(fin_ready, g + 1)
                sp.dma_start(out_rows[:, g * CT:(g + 1) * CT, :], fin[:, g * CT:(g + 1) * CT, :]).then_inc(fin_out, 16)
            sp.wait_ge(fin_out, 16 * (TILES // CT))
            sp.wait_ge(xt_in, 16 * XS_TILES)

        @block.gpsimd
        def _(pool):
            pool.memset(zero_t, 0.0).then_inc(zero_made, 1)
            pool.memset(mhalf[:, :], -0.5).then_inc(made, 1)
            pool.memset(ident[:, :], 0.0).then_inc(made, 1)
            pool.memset(eye4[:, :, :], 0.0).then_inc(made, 1)
            pool.memset(hmask, 1.0).then_inc(made, 1)
            pool.memset(one_c[:, :], 1.0).then_inc(made, 1)
            pool.wait_ge(made, 5)
            pool.affine_select(out=ident[:, :], in_=ident[:, :], compare_op=ALU.not_equal, fill=1.0, base=0,
                               pattern=[[-1, P]], channel_multiplier=1).then_inc(made, 1)
            pool.affine_select(out=eye4[:, :, :], in_=eye4[:, :, :], compare_op=ALU.not_equal, fill=1.0, base=0,
                               pattern=[[0, HG], [-1, SC]], channel_multiplier=1).then_inc(made, 1)
            pool.affine_select(out=hmask, in_=hmask, compare_op=ALU.is_ge, fill=0.0, base=0,
                               pattern=[[-DK, HC]], channel_multiplier=1).then_inc(made, 1)
            pool.wait_ge(made, 8)
            pool.affine_select(out=hmask, in_=hmask, compare_op=ALU.is_ge, fill=0.0, base=DK - 1,
                               pattern=[[DK, HC]], channel_multiplier=-1).then_inc(made, 1)

            with pool.Fori(0, CHUNKS) as it:
                for n in range(3):
                    pool.wait_ge(ln_var, it * 3 + n + 1)
                    pool.tensor_tensor(rstd[:, :], veps[:, :], mhalf[:, :], ALU.pow).then_inc(ln_rstd, 1)
                pool.wait_ge(pads_zeroed, 16)
                pool.wait_ge(x2_ready, it + 1)
                pool.tensor_copy(X2[:, bass.ds(it * CT, CT), :], x2c).then_inc(x2_kept, 1)

            pool.wait_ge(lg_ready, CHUNKS)
            pool.iota(tau, pattern=[[1, XS_TILES], [0, E]], base=0, channel_multiplier=0,
                      allow_small_or_imprecise_dtypes=True).then_inc(route_consts, 1)
            pool.iota(rev, pattern=[[-1, E]], base=E, channel_multiplier=0,
                      allow_small_or_imprecise_dtypes=True).then_inc(route_consts, 1)
            pool.memset(ones_m, 1.0).then_inc(route_consts, 1)
            pool.memset(ones_r, 1.0).then_inc(route_consts, 1)
            pool.wait_ge(route_consts, 4)
            pool.affine_select(out=tri, in_=ones_m, compare_op=ALU.is_gt, fill=0.0, base=0,
                               pattern=[[1, P]], channel_multiplier=-1).then_inc(route_consts, 1)

            pool.wait_ge(pads_zeroed, 16)
            pool.wait_ge(slots_ready, TOPK)
            for t in range(TILES):
                for c in range(TOPK):
                    pool.indirect_dma_start(xs, bass.IndirectOffsetOnAxis(where[c][:, t:t + 1], 0), X2[:, t, :],
                                            None).then_inc(scattered, 16)
            pool.wait_ge(y_out, 16 * SLOT_TILES)
            for t in range(TILES):
                for c in range(TOPK):
                    pool.indirect_dma_start(y_of[c][:, t, :], None, ys,
                                            bass.IndirectOffsetOnAxis(where[c][:, t:t + 1], 0)).then_inc(gathered[t], 16)
                if t % CT == CT - 1 and t >= 2 * CT - 1:
                    for n in range(2):
                        k = 2 * (t // CT - 1) + n
                        pool.wait_ge(f_var, k + 1)
                        pool.tensor_tensor(rstd[:, :], veps[:, :], mhalf[:, :], ALU.pow).then_inc(f_rstd, 1)
            for n in range(2):
                k = 2 * (TILES // CT - 1) + n
                pool.wait_ge(f_var, k + 1)
                pool.tensor_tensor(rstd[:, :], veps[:, :], mhalf[:, :], ALU.pow).then_inc(f_rstd, 1)

        @block.scalar
        def _(act):
            act.wait_ge(consts_in, 5 * 16)
            act.mul(bka_s[:, :], bka_s[:, :], D ** -0.5).then_inc(bka_ready, 1)
            act.wait_ge(bka_ready, 1)
            with act.Fori(0, CHUNKS) as it:
                act.wait_ge(hT_mm, it + 1)
                for k in range(KD):
                    last = act.activation(hT[:, k, :], pa[:, k, :], ACT.Identity, scale=gam[:, k:k + 1],
                                          bias=bet[:, k:k + 1])
                last.then_inc(hT_ready, 1)
                act.wait_ge(k_mm, it + 1)
                for k in range(KD):
                    last = act.activation(keysT[:, k, :], pb[:, k, :], ACT.Identity, bias=bk_s[:, k:k + 1])
                last.then_inc(kT_ready, 1)
                act.wait_ge(ka_mm, it + 1)
                for k in range(KD):
                    act.activation(kexp[:, k, :], pa[:, k, :], ACT.Exp, scale=D ** -0.5,
                                   bias=bka_s[:, k:k + 1]).then_inc(kexp_ready, 1)
                act.wait_ge(x1T_mm, it + 1)
                act.activation(x1T, pa[:, :, :], ACT.Copy).then_inc(x1T_ready, 1)
                act.wait_ge(q_mm, it + 1)
                act.activation(qT, pb[:, :, :], ACT.Copy).then_inc(qT_ready, 1)

                def copy_probT(u):
                    act.wait_ge(pT_mm, (it * UNITS + u) * 2 + 1)
                    act.activation(probT[0:SC, u % 2, 0:HG, :], pc[0:SC, 0, :].rearrange("p (h q) -> p h q", h=HG),
                                   ACT.Copy).then_inc(pT_ready, 1)

                def copy_mergedT(j):
                    act.wait_ge(mT_mm, it * CT + j + 1)
                    act.activation(mergedT[:, j % 2], pm[:, 0:D].rearrange("p (k q) -> p k q", k=KD),
                                   ACT.Copy).then_inc(mT_ready, 1)

                for u in range(UNITS):
                    act.wait_ge(sub_ready, it * UNITS + u + 1)
                    act.activation(prob[:, u % 2], prob[:, u % 2], ACT.Exp, scale=DK ** -0.5).then_inc(exp_ready, 1)
                    if u >= 1:
                        copy_probT(u - 1)
                    if u >= 4 and u % 2 == 0:
                        copy_mergedT(u // 2 - 2)
                copy_probT(UNITS - 1)
                copy_mergedT(CT - 2)
                copy_mergedT(CT - 1)
                act.wait_ge(x2T_mm, it + 1)
                act.activation(x2T, pa[:, :, :], ACT.Copy).then_inc(x2T_ready, 1)

            act.wait_ge(route, ROUTE_DIFF)
            act.activation(ex, ex, ACT.Exp).then_inc(ex_ready, 1)

            with act.Fori(0, SLOT_TILES) as t:
                for n in range(2):
                    act.wait_ge(hb_ready, t * 2 + n + 1)
                    act.activation(hg[:, n * 512:(n + 1) * 512], hb[:, n * 512:(n + 1) * 512],
                                   ACT.Gelu).then_inc(hg_ready, 1)
                act.wait_ge(hgT_mm, t * 2 + 1)
                act.activation(hgT[:, 0:KF // 2, :], pb[:, 0, :].rearrange("p (k q) -> p k q", k=KF // 2),
                               ACT.Copy).then_inc(hgT_ready, 1)

        @block.vector
        def _(dve):
            def layer_norm(src, dst, eps, done, n, var_sem, rstd_sem, ready):
                for j in range(CT):
                    last = dve.bn_stats(stats[:, j, :], src[:, j, :])
                last.then_inc(ln_stats, 1)
                mean_e, mean_o, var_e, var_o = stats[:, :, 1], stats[:, :, 4], stats[:, :, 2], stats[:, :, 5]
                dve.wait_ge(ln_stats, n + 1)
                dve.tensor_tensor(mdiff[:, :], mean_e, mean_o, ALU.subtract)
                dve.tensor_tensor(msum[:, :], mean_e, mean_o, ALU.add)
                dve.scalar_tensor_tensor(vsum[:, :], var_e, D * eps, var_o, ALU.add, ALU.add).then_inc(ln_mv, 1)
                dve.wait_ge(ln_mv, 2 * n + 1)
                dve.scalar_tensor_tensor(msq[:, :], mdiff[:, :], 0.25, mdiff[:, :], ALU.mult, ALU.mult)
                dve.tensor_scalar(mean[:, :], msum[:, :], 0.5, None, ALU.mult).then_inc(ln_mv, 1)
                dve.wait_ge(ln_mv, 2 * n + 2)
                dve.scalar_tensor_tensor(veps[:, :], vsum[:, :], 1.0 / D, msq[:, :], ALU.mult, ALU.add).then_inc(var_sem, 1)
                dve.wait_ge(rstd_sem, ready)
                for j in range(CT):
                    last = dve.tensor_scalar(dst[:, j, :], src[:, j, :], mean[:, j:j + 1], rstd[:, j:j + 1],
                                             ALU.subtract, ALU.mult)
                last.then_inc(done, 1)

            dve.wait_ge(ctx_in, 8 * 16)
            dve.tensor_scalar(mask_b[0:SC, :], mask_raw, MASKED, None, ALU.mult).then_inc(mask_made, 1)
            dve.memset(vaug[0:SC], 1.0).then_inc(mask_made, 1)
            dve.wait_ge(made, MADE)
            dve.wait_ge(mask_made, 2)
            dve.wait_ge(ctx_mm, 1)
            for c in range(KD):
                for b in range(B):
                    keys = pa[:, c, b * SC:(b + 1) * SC].rearrange("p (h k) -> p h k", h=1).to_broadcast([P, HC, SC])
                    dve.tensor_tensor(kbd[:, b, c], keys, hmask.rearrange("p (h k) -> p h k", k=1).to_broadcast([P, HC, SC]),
                                      ALU.mult)
            for b in range(B):
                last = dve.tensor_copy(vaug[0:SC, b, :, 0:DK], pb[0:SC, b, 0:D].rearrange("p (h v) -> p h v", h=HEADS))
            last.then_inc(kv_made, 1)

            one_s = one_c[:, 0:1].to_broadcast([P, CHUNK])
            with dve.Fori(0, B) as b:
                dve.memset(csum[:, :, CHUNK - 1:CHUNK], 0.0)
                dve.memset(pooled[:, :, CHUNK - 1:CHUNK], 0.0).then_inc(carry_reset, 1)
                with dve.Fori(0, CPB) as c:
                    it = b * CPB + c
                    dve.wait_ge(x_in, it * 16 + 16)
                    layer_norm(xc, h0, EPS, h0_ready, it * 3, ln_var, ln_rstd, it * 3 + 1)
                    dve.wait_ge(carry_reset, b + 1)
                    for k in range(KD):
                        dve.wait_ge(kexp_ready, it * KD + k + 1)
                        dve.tensor_tensor_scan(csum[:, k, :], one_s, kexp[:, k, :], csum[:, k, CHUNK - 1:CHUNK],
                                               ALU.mult, ALU.add).then_inc(scanned, 1)
                    dve.wait_ge(scanned, it * 2 * KD + KD)
                    dve.reciprocal(kw, csum).then_inc(recip_ready, 1)
                    dve.wait_ge(recip_ready, it + 1)
                    dve.tensor_tensor(kw, kw, kexp, ALU.mult).then_inc(kw_part, 1)
                    dve.wait_ge(kw_part, it + 1)
                    dve.tensor_tensor(kw, kw, keysT, ALU.mult).then_inc(kw_ready, 1)
                    dve.wait_ge(kw_ready, it + 1)
                    for k in range(KD):
                        dve.tensor_tensor_scan(pooled[:, k, :], one_s, kw[:, k, :], pooled[:, k, CHUNK - 1:CHUNK],
                                               ALU.mult, ALU.add).then_inc(scanned, 1)
                    dve.wait_ge(scanned, it * 2 * KD + 2 * KD)
                    dve.wait_ge(v_mm, it + 1)
                    for k in range(KD):
                        last = dve.scalar_tensor_tensor(attnT[:, k, :], pc[:, k, :], bv_s[:, k:k + 1], pooled[:, k, :],
                                                        ALU.add, ALU.mult)
                    last.then_inc(attn_ready, 1)
                    dve.wait_ge(at_mm, it + 1)
                    dve.tensor_tensor(h0, pb_t, xc, ALU.add).then_inc(x_free, 1)
                    dve.wait_ge(x_free, it + 1)
                    layer_norm(h0, x1, EPS, x1_ready, it * 3 + 1, ln_var, ln_rstd, it * 3 + 2)

                    def residual(j):
                        dve.wait_ge(o_mm, it * CT + j + 1)
                        dve.tensor_tensor(h0[:, j, :], pm[:, D:2 * D], x1[:, j, :], ALU.add).then_inc(r2_ready, 1)

                    def normalise_heads(j):
                        dve.wait_ge(pv_mm, it * CT + j + 1)
                        sums = pv[:, 0:HEADS * VW].rearrange("p (h v) -> p h v", h=HEADS)
                        dve.reciprocal(psum_r[:, :], sums[:, :, DK]).then_inc(rec_ready, 1)
                        dve.wait_ge(rec_ready, it * CT + j + 1)
                        dve.scalar_tensor_tensor(pscale[:, :], smax[:, j % 2, :], MASKED / 10, psum_r[:, :], ALU.is_gt,
                                                 ALU.mult).then_inc(scale_ready, 1)
                        dve.wait_ge(scale_ready, it * CT + j + 1)
                        dve.tensor_tensor(merged[:, j % 2, :].rearrange("p (h v) -> p h v", h=HEADS), sums[:, :, 0:DK],
                                          pscale[:, :].rearrange("p (h v) -> p h v", v=1).to_broadcast([P, HEADS, DK]),
                                          ALU.mult).then_inc(merged_ready, 1)

                    def copy_probT(u):
                        dve.wait_ge(pT_mm, (it * UNITS + u) * 2 + 2)
                        dve.tensor_copy(probT[0:SC, u % 2, HG:HC, :],
                                        pc[0:SC, 1, :].rearrange("p (h q) -> p h q", h=HG)).then_inc(pT_ready, 1)

                    for u in range(UNITS):
                        j, half = divmod(u, KD)
                        s_h = score[u % 2][:, :, 0:HG * SC].rearrange("p g (h k) -> p g h k", h=HG)
                        top = smax[:, j % 2, half * HC:(half + 1) * HC]
                        dve.wait_ge(s_mm, it * UNITS + u + 1)
                        dve.tensor_reduce(top.rearrange("p (g h) -> p g h", g=KD), s_h, AX.X, ALU.max).then_inc(max_ready, 1)
                        dve.wait_ge(max_ready, it * UNITS + u + 1)
                        if u >= 2:
                            dve.wait_ge(pT_mm, (it * UNITS + u) * 2 - 2)
                        dve.tensor_tensor(prob[:, u % 2].rearrange("p (g h) k -> p g h k", g=KD), s_h,
                                          top.rearrange("p (g h k) -> p g h k", g=KD, k=1).to_broadcast([P, KD, HG, SC]),
                                          ALU.subtract).then_inc(sub_ready, 1)
                        if u >= 1:
                            copy_probT(u - 1)
                        if u >= 5 and u % 2 == 1:
                            residual((u - 5) // 2)
                        if u >= 3 and u % 2 == 1:
                            normalise_heads((u - 3) // 2)
                    copy_probT(UNITS - 1)
                    residual(CT - 2)
                    normalise_heads(CT - 1)
                    residual(CT - 1)
                    dve.wait_ge(r2_ready, it * CT + CT)
                    layer_norm(h0, x2c, EPS, x2_ready, it * 3 + 2, ln_var, ln_rstd, it * 3 + 3)
                    dve.wait_ge(lg_mm, it + 1)
                    dve.wait_ge(x2_kept, it + 1)
                    dve.tensor_tensor(logits[:, bass.ds(it * CT, CT), :], pm[:, 0:CT * E].rearrange("p (j e) -> p j e", j=CT),
                                      rb_s.rearrange("p (j e) -> p j e", j=1).to_broadcast([P, CT, E]),
                                      ALU.add).then_inc(lg_ready, 1)

            steps = [0]

            def then(ins):
                steps[0] += 1
                ins.then_inc(route, 1)
                dve.wait_ge(route, steps[0])

            def per_e(ap):
                return ap.rearrange("p (a e) -> p a e", a=1).to_broadcast([P, TILES, E])

            def per_t(ap):
                return ap.rearrange("p (t e) -> p t e", e=1).to_broadcast([P, TILES, E])

            dve.wait_ge(lg_ready, CHUNKS)
            dve.wait_ge(route_consts, 5)
            lg = logits[:, :, :]
            for c, (src, top) in enumerate(((lg, m1), (rest, m2))):
                then(dve.tensor_reduce(top, src, AX.X, ALU.max))
                then(dve.tensor_tensor(cand, src, per_t(top), ALU.is_equal))
                then(dve.tensor_tensor(cand, cand, per_e(rev), ALU.mult))
                then(dve.tensor_reduce(first, cand, AX.X, ALU.max))
                then(dve.tensor_tensor(hot[c], cand, per_t(first), ALU.is_equal))
                if c == 0:
                    then(dve.scalar_tensor_tensor(rest, hot[0], -3e38, lg, ALU.mult, ALU.add))
            then(dve.tensor_tensor(both, hot[0], hot[1], ALU.add))
            assert steps[0] == ROUTE_BOTH
            then(dve.tensor_tensor(ex, m2, m1, ALU.subtract))
            assert steps[0] == ROUTE_DIFF
            dve.wait_ge(count_mm, 1)
            then(dve.tensor_copy(tot, pv[:, P:2 * P].rearrange("p (t e) -> p e t", e=E)))
            then(dve.tensor_tensor_scan(run.rearrange("p e t -> p (e t)"), ones_r, tot.rearrange("p e t -> p (e t)"), 0.0,
                                        ALU.mult, ALU.add))
            then(dve.memset(starts[:, 0:1], 0.0))
            then(dve.tensor_copy(starts[:, 1:E], run[:, 0:E - 1, TILES - 1]))
            then(dve.tensor_tensor(count, run[:, :, TILES - 1], starts, ALU.subtract))
            then(dve.tensor_scalar(counti.bitcast(I32), count, float(P - 1), None, ALU.add))
            then(dve.tensor_scalar(counti.bitcast(I32), counti.bitcast(I32), 7, None, ALU.logical_shift_right))
            then(dve.tensor_copy(ntile, counti.bitcast(I32)))
            then(dve.tensor_tensor_scan(tbend, ones_r[:, 0:E], ntile, 0.0, ALU.mult, ALU.add))
            then(dve.tensor_tensor(adj, tbend, ntile, ALU.subtract))
            then(dve.scalar_tensor_tensor(adj, adj, float(P), starts, ALU.mult, ALU.subtract))
            then(dve.tensor_tensor(run, run, tot, ALU.subtract))
            then(dve.tensor_tensor(run, run, adj.rearrange("p (e t) -> p e t", t=1).to_broadcast([P, E, TILES]), ALU.add))
            then(dve.tensor_tensor(slots, pv[:, 0:P].rearrange("p (t e) -> p t e", e=E),
                                   run.rearrange("p e t -> p t e"), ALU.add))
            for c in range(TOPK):
                then(dve.tensor_tensor(picked, slots, hot[c], ALU.mult))
                then(dve.tensor_reduce(slotf, picked, AX.X, ALU.add))
                dve.tensor_copy(where[c][:, :], slotf).then_inc(slots_ready, 1)
            dve.wait_ge(slots_ready, TOPK)
            then(dve.tensor_tensor(tge, tau, tbend.rearrange("p (t e) -> p t e", t=1).to_broadcast([P, XS_TILES, E]),
                                   ALU.is_ge))
            then(dve.tensor_reduce(tilef, tge, AX.X, ALU.add))
            dve.tensor_scalar(expert_of[:, :], tilef, float(E - 1), None, ALU.min).then_inc(table_ready, 1)
            dve.wait_ge(table_ready, 1)
            dve.wait_ge(ex_ready, 1)
            then(dve.tensor_scalar(den, ex, 1.0, None, ALU.add))
            then(dve.reciprocal(weight[0][:, :], den))
            then(dve.tensor_tensor(weight[1][:, :], weight[0][:, :], ex, ALU.mult))
            assert steps[0] == ROUTE_STEPS

            dve.wait_ge(late_in, 2 * 16)

            def copy_xtT(n):
                dve.wait_ge(xt_mm, n)
                dve.tensor_copy(xtT, pm[:, 0:D].rearrange("p (k q) -> p k q", k=KD)).then_inc(xt_ready, 1)

            def hidden(t, e):
                for n in range(2):
                    dve.wait_ge(h_mm, t * 2 + n + 1)
                    dve.tensor_tensor(hb[:, n * 512:(n + 1) * 512], pa[:, n, :],
                                      b1_s[:, bass.ds(e, 1), n * 512:(n + 1) * 512].rearrange("p a f -> p (a f)"),
                                      ALU.add).then_inc(hb_ready, 1)
                copy_xtT(t + 2)

            def copy_hgT(t):
                dve.wait_ge(hgT_mm, t * 2 + 2)
                dve.tensor_copy(hgT[:, KF // 2:KF, :],
                                pb[:, 1, :].rearrange("p (k q) -> p k q", k=KF // 2)).then_inc(hgT_ready, 1)

            def finish_tile(n, e):
                dve.wait_ge(y_mm, n)
                dve.tensor_tensor(yt, pv[:, 0:D], b2_s[:, bass.ds(e, 1), :].rearrange("p a d -> p (a d)"),
                                  ALU.add).then_inc(y_ready, 1)

            def expert(t):
                return nc.values_load(expert_of[0:1, bass.ds(t, 1)], engines=[mybir.EngineType.DVE], min_val=0, max_val=E - 1,
                                      skip_runtime_bounds_check_because="the table is clamped to the experts")

            copy_xtT(1)
            hidden(0, expert(0))
            copy_hgT(0)
            with dve.Fori(1, SLOT_TILES) as t:
                e_before = expert(t - 1)
                hidden(t, expert(t))
                finish_tile(t, e_before)
                copy_hgT(t)
                dve.wait_ge(y_out, t * 16)
            finish_tile(SLOT_TILES, expert(SLOT_TILES - 1))

            dve.wait_ge(ln_in, 2 * 16)
            fs = [0]

            def step(ins):
                fs[0] += 1
                ins.then_inc(fin_step, 1)
                dve.wait_ge(fin_step, fs[0])

            for g in range(TILES // CT):
                for j in range(CT):
                    t = g * CT + j
                    dve.wait_ge(gathered[t], TOPK * 16)
                    last = dve.scalar_tensor_tensor(acc[:, j, :], y_of[0][:, t, :], weight[0][:, t:t + 1], X2[:, t, :],
                                                    ALU.mult, ALU.add)
                step(last)
                for j in range(CT):
                    t = g * CT + j
                    last = dve.scalar_tensor_tensor(acc[:, j, :], y_of[1][:, t, :], weight[1][:, t:t + 1], acc[:, j, :],
                                                    ALU.mult, ALU.add)
                step(last)
                layer_norm(acc, zed, EPS_FFN, fin_step, 3 * CHUNKS + 2 * g, f_var, f_rstd, 2 * g + 1)
                fs[0] += 1
                dve.wait_ge(fin_step, fs[0])
                step(dve.tensor_tensor(zed, zed, lnw_s.rearrange("p (j d) -> p j d", j=1).to_broadcast([P, CT, D]), ALU.mult))
                step(dve.tensor_tensor(zed, zed, lnb_s.rearrange("p (j d) -> p j d", j=1).to_broadcast([P, CT, D]), ALU.add))
                step(dve.tensor_tensor(zed, zed, X2[:, g * CT:(g + 1) * CT, :], ALU.add))
                layer_norm(zed, fin[:, g * CT:(g + 1) * CT, :], EPS, fin_ready, 3 * CHUNKS + 2 * g + 1, f_var, f_rstd, 2 * g + 2)

        @block.tensor
        def _(pe):
            pe.wait_ge(ctx_in, 8 * 16)
            for c in range(KD):
                for k in range(KD):
                    pe.matmul(pa[:, c, 0:B * SC], wxk_s[:, k, c * P:(c + 1) * P], ctx_s[:, k, :], start=(k == 0),
                              stop=(k == KD - 1))
            for b in range(B):
                for k in range(KD):
                    last = pe.matmul(pb[0:SC, b, 0:D], ctx_s[:, k, b * SC:(b + 1) * SC], wxv_s[:, k, :], start=(k == 0),
                                     stop=(k == KD - 1))
            last.then_inc(ctx_mm, 1)
            pe.wait_ge(weights_in, 3 * 16)
            pe.wait_ge(made, MADE)
            pe.wait_ge(kv_made, 1)

            def project(dst, w, src):
                for c in range(KD):
                    for k in range(KD):
                        last = pe.matmul(dst[:, c, :], w[:, k, c * P:(c + 1) * P], src[:, k, :], start=(k == 0),
                                         stop=(k == KD - 1))
                return last

            def to_features(dst, src):
                for j in range(CT):
                    for k in range(KD):
                        last = pe.transpose(dst[:, k, j * P:(j + 1) * P], src[:, j, k * P:(k + 1) * P], ident[:, :])
                return last

            with pe.Fori(0, B) as b:
                with pe.Fori(0, CPB) as c:
                    it = b * CPB + c
                    pe.wait_ge(h0_ready, it + 1)
                    to_features(pa, h0).then_inc(hT_mm, 1)
                    pe.wait_ge(hT_ready, it + 1)
                    project(pb, wk_s, hT).then_inc(k_mm, 1)
                    pe.wait_ge(kT_ready, it + 1)
                    project(pa, wka_s, keysT).then_inc(ka_mm, 1)
                    project(pc, wv_s, hT).then_inc(v_mm, 1)
                    pe.wait_ge(attn_ready, it + 1)
                    for j in range(CT):
                        for k in range(KD):
                            last = pe.transpose(pb_t[:, j, k * P:(k + 1) * P], attnT[:, k, j * P:(j + 1) * P], ident[:, :])
                    last.then_inc(at_mm, 1)
                    pe.wait_ge(x1_ready, it + 1)
                    to_features(pa, x1).then_inc(x1T_mm, 1)
                    pe.wait_ge(x1T_ready, it + 1)
                    project(pb, wq_s, x1T).then_inc(q_mm, 1)
                    pe.wait_ge(qT_ready, it + 1)

                    def scores(u):
                        j, half = divmod(u, KD)
                        if u >= 2:
                            pe.wait_ge(sub_ready, it * UNITS + u - 1)
                        for g in range(KD):
                            dst = score[u % 2][:, g, 0:HG * SC]
                            pe.matmul(dst, qT[:, half, j * P:(j + 1) * P],
                                      kbd[:, bass.ds(b, 1), half, g * HG:(g + 1) * HG, :].rearrange("p a h k -> p (a h k)"),
                                      start=True, stop=False)
                            last = pe.matmul(dst, mask_b[0:SC, bass.ds(c * CHUNK + j * P, P)],
                                             eye4[0:SC, :, :].rearrange("p h k -> p (h k)"), start=False, stop=True)
                        last.then_inc(s_mm, 1)

                    def turn_probs(u):
                        pe.wait_ge(exp_ready, it * UNITS + u + 1)
                        if u >= 1:
                            pe.wait_ge(pT_ready, (it * UNITS + u) * 2)
                        for h in range(HC):
                            last = pe.transpose(pc[0:SC, h // HG, (h % HG) * P:(h % HG + 1) * P], prob[:, u % 2, h, :],
                                                ident[:, :])
                            if h % HG == HG - 1:
                                last.then_inc(pT_mm, 1)

                    def weigh_values(u):
                        j, half = divmod(u, KD)
                        pe.wait_ge(pT_ready, (it * UNITS + u) * 2 + 2)
                        if half == 0 and j >= 1:
                            pe.wait_ge(merged_ready, it * CT + j)
                        for n in range(HC):
                            h = half * HC + n
                            last = pe.matmul(pv[:, h * VW:(h + 1) * VW], probT[0:SC, u % 2, n, :],
                                             vaug[0:SC, bass.ds(b, 1), h, :].rearrange("p a v -> p (a v)"),
                                             start=True, stop=True)
                        if half == KD - 1:
                            last.then_inc(pv_mm, 1)

                    def project_out(j):
                        pe.wait_ge(merged_ready, it * CT + j + 1)
                        for k in range(KD):
                            last = pe.transpose(pm[:, k * P:(k + 1) * P], merged[:, j % 2, k * P:(k + 1) * P], ident[:, :])
                        last.then_inc(mT_mm, 1)
                        pe.wait_ge(mT_ready, it * CT + j + 1)
                        if j >= 1:
                            pe.wait_ge(r2_ready, it * CT + j)
                        for k in range(KD):
                            last = pe.matmul(pm[:, D:2 * D], mergedT[:, j % 2, k, :], wo_s[:, k, :], start=(k == 0),
                                             stop=(k == KD - 1))
                        last.then_inc(o_mm, 1)

                    scores(0)
                    scores(1)
                    turn_probs(0)
                    for u in range(UNITS):
                        if u + 2 < UNITS:
                            scores(u + 2)
                        if u + 1 < UNITS:
                            turn_probs(u + 1)
                        weigh_values(u)
                        if u >= 3 and u % 2 == 1:
                            project_out((u - 3) // 2)
                    project_out(CT - 1)

                    pe.wait_ge(x2_ready, it + 1)
                    to_features(pa, x2c).then_inc(x2T_mm, 1)
                    pe.wait_ge(x2T_ready, it + 1)
                    for j in range(CT):
                        for k in range(KD):
                            last = pe.matmul(pm[:, j * E:(j + 1) * E], x2T[:, k, j * P:(j + 1) * P], rw_s[:, k, :],
                                             start=(k == 0), stop=(k == KD - 1))
                    last.then_inc(lg_mm, 1)

            pe.wait_ge(route_consts, 5)
            pe.wait_ge(route, ROUTE_BOTH)
            chosen = both.rearrange("p t e -> p (t e)")
            pe.matmul(pv[:, 0:P], tri, chosen, start=True, stop=True)
            pe.matmul(pv[:, P:2 * P], ones_m, chosen, start=True, stop=True).then_inc(count_mm, 1)

            def expert(t):
                return nc.values_load(expert_of[0:1, bass.ds(t, 1)], engines=[mybir.EngineType.PE], min_val=0, max_val=E - 1,
                                      skip_runtime_bounds_check_because="the table is clamped to the experts")

            def turn_rows(n):
                pe.wait_ge(xt_in, n * 16)
                for k in range(KD):
                    last = pe.transpose(pm[:, k * P:(k + 1) * P], xt[:, k * P:(k + 1) * P], ident[:, :])
                last.then_inc(xt_mm, 1)

            def up(t, e):
                pe.wait_ge(xt_ready, t + 1)
                for n in range(2):
                    for k in range(KD):
                        last = pe.matmul(pa[:, n, :], xtT[:, k, :],
                                         w1_v[:, bass.ds(e, 1), k, n * 512:(n + 1) * 512].rearrange("p a f -> p (a f)"),
                                         start=(k == 0), stop=(k == KD - 1))
                    last.then_inc(h_mm, 1)

            def down(n, e):
                pe.wait_ge(hgT_ready, n * 2)
                for k in range(KF):
                    last = pe.matmul(pv[:, 0:D], hgT[:, k, :], w2_v[:, bass.ds(e, 1), k, :].rearrange("p a d -> p (a d)"),
                                     start=(k == 0), stop=(k == KF - 1))
                last.then_inc(y_mm, 1)

            def turn_hidden(t):
                for n in range(2):
                    pe.wait_ge(hg_ready, t * 2 + n + 1)
                    for k in range(KF // 2):
                        q = n * (KF // 2) + k
                        last = pe.transpose(pb[:, n, k * P:(k + 1) * P], hg[:, q * P:(q + 1) * P], ident[:, :])
                    last.then_inc(hgT_mm, 1)

            pe.wait_ge(table_ready, 1)
            turn_rows(1)
            pe.wait_ge(experts_in, 2 * E * 16)
            up(0, expert(0))
            turn_rows(2)
            turn_hidden(0)
            with pe.Fori(1, SLOT_TILES) as t:
                e_before = expert(t - 1)
                e = expert(t)
                up(t, e)
                turn_rows(t + 2)
                down(t, e_before)
                turn_hidden(t)
            down(SLOT_TILES, expert(SLOT_TILES - 1))


MADE = 9
ROUTE_BOTH = 12
ROUTE_DIFF = 13
ROUTE_STEPS = ROUTE_DIFF + 14 + 2 * TOPK + 2 + 3


def kernel(**inputs):
    import numpy as np
    import concourse.bacc as bacc
    from concourse.bass_utils import run_bass_kernel_spmd

    def a(name, pre="L0_"):
        return np.asarray(inputs[pre + name])

    def turned(w, *axes):
        return np.ascontiguousarray(w.transpose(*axes)) if axes else np.ascontiguousarray(w.T)

    mask = a("mask_1x1xSxS2_bk1", "").reshape(S, SC)
    arrays = {
        "x": np.ascontiguousarray(a("x", "").reshape(T, D)),
        "ctxT": turned(a("ctx_1024", "").reshape(B * SC, D)),
        "maskT": turned(mask),
        "wk": turned(a("attn_Wk")), "bk": a("attn_bk"), "wka": turned(a("attn_Wka")), "bka": a("attn_bka"),
        "wv": turned(a("attn_Wv")), "bv": a("attn_bv"), "gamma": a("attn_gamma"), "beta": a("attn_beta"),
        "wq": turned(a("xattn_W_q")), "wxk": turned(a("xattn_W_k")), "wxv": turned(a("xattn_W_v")), "wo": turned(a("xattn_W_o")),
        "rw": turned(a("ffn_router_w")), "rb": a("ffn_router_b"),
        "w1": turned(a("ffn_w1"), 0, 2, 1), "b1": a("ffn_b1"), "w2": turned(a("ffn_w2"), 0, 2, 1), "b2": a("ffn_b2"),
        "lnw": a("ffn_ln_w"), "lnb": a("ffn_ln_b"),
    }
    nc = bacc.Bacc("TRN2", target_bir_lowering=False, num_devices=1)
    args = {n: nc.dram_tensor(f"in_{n}", v.shape, mybir.dt.from_np(v.dtype), kind="ExternalInput").ap()
            for n, v in arrays.items()}
    result = nc.dram_tensor("out", (T, D), F32, kind="ExternalOutput").ap()
    decoder_layer(nc, out=result, **args)
    r = run_bass_kernel_spmd(nc, [{f"in_{n}": v for n, v in arrays.items()}], core_ids=[0])
    return np.asarray(r.results[0]["out"]).reshape(B, S, D)
```

```python
from contextlib import ExitStack

import concourse.bass as bass
from concourse import mybir

F32 = mybir.dt.float32
BF16 = mybir.dt.bfloat16
I32 = mybir.dt.int32
U32 = mybir.dt.uint32
U8 = mybir.dt.uint8
ALU = mybir.AluOpType
ACT = mybir.ActivationFunctionType
AX = mybir.AxisListType

P = 128
B, S, D = 2, 1024, 256
T = B * S
KD = D // P
TILES = T // P
CT = 4
CHUNK = CT * P
CPB = S // CHUNK
CHUNKS = T // CHUNK
SC = 77
HEADS, DK = 16, 16
HC = P // DK
HG = 4
VW = DK + 1
E, FF = 8, 1024
KF = FF // P
TOPK = 2
SLOT_TILES = TOPK * T // P + E - 1
XS_TILES = SLOT_TILES + 1
EPS = 1e-5
EPS_FFN = 1e-12
MASKED = -1e30
QUADS = HEADS // 4
STEPS = CT * QUADS
RING = 4
CARRIES = 2 * CHUNKS + 1
GROUPS = TILES // CT


def decoder_layer(nc, x, ctxT, maskT, wk, bk, wka, bka, wv, bv, gamma, beta, wq, wxk, wxv, wo,
                  rw, rb, w1, b1, w2, b2, lnw, lnb, out):
    xs = nc.dram_tensor("sorted_tokens", [XS_TILES * P, D], F32).ap()
    ys = nc.dram_tensor("sorted_outputs", [SLOT_TILES * P, D], F32).ap()

    x_rows = x.rearrange("(t p) d -> p t d", p=P)
    out_rows = out.rearrange("(t p) d -> p t d", p=P)
    xs_tiles = xs.rearrange("(t p) d -> p t d", p=P)
    ys_tiles = ys.rearrange("(t p) d -> p t d", p=P)

    with ExitStack() as ctx:
        def sb(name, shape, dt=F32):
            return ctx.enter_context(nc.sbuf_tensor(name, shape, dt))

        def sem(name):
            return ctx.enter_context(nc.semaphore(name))

        W1 = sb("expert_w1", [P, E * KD * FF])
        W2 = sb("expert_w2", [P, E * KF * D])
        LATE = sb("front_weights_then_b1", [P, E * FF])
        X2 = sb("x2", [P, TILES, D])
        R = sb("work", [P, 5888])
        w1_v = W1[:, :].rearrange("p (e k f) -> p e k f", e=E, k=KD)
        w2_v = W2[:, :].rearrange("p (e k n) -> p e k n", e=E, k=KF)
        EW = KD * FF
        EARLY = 5

        def slot(n):
            t, m = (W1, n) if n < 6 else (W2, n - 6)
            return t[:, EARLY * EW + m * 1024:EARLY * EW + (m + 1) * 1024]

        def by_tile(ap):
            return ap.rearrange("p (j d) -> p j d", j=CT)

        def by_chunk(ap):
            return ap.rearrange("p (k n) -> p k n", k=KD)

        xc = by_tile(slot(0))
        h0 = by_tile(slot(1))
        hT = by_chunk(slot(2))
        x1T = by_chunk(slot(2))
        keysT = by_chunk(slot(3))
        kexp = by_chunk(slot(4))
        csum = by_chunk(slot(5))
        kw = by_chunk(slot(6))
        attnT = by_chunk(slot(6))
        pooled = by_chunk(slot(7))
        r2 = by_tile(slot(8))
        x1 = by_tile(slot(9))
        x2c = by_tile(slot(10))
        qT = by_chunk(slot(11))

        off = [0]

        def late(n):
            off[0] += n
            return LATE[:, off[0] - n:off[0]]

        def late_w():
            return late(KD * D).rearrange("p (k n) -> p k n", k=KD)

        wk_s, wka_s, wv_s, wq_s, wo_s, wxk_s, wxv_s = (late_w() for _ in range(7))
        kbd = late(B * HEADS * SC).rearrange("p (b c h k) -> p b c h k", b=B, c=KD, h=HC)
        vaug = late(B * HEADS * VW).rearrange("p (b h v) -> p b h v", b=B, h=HEADS)
        ctx_s = late(KD * B * SC).rearrange("p (k n) -> p k n", k=KD)
        rw_s = late(KD * E).rearrange("p (k e) -> p k e", k=KD)
        rb_s = late(E)
        assert off[0] <= E * FF
        b1_s = LATE[:, :].rearrange("p (e f) -> p e f", e=E)

        prob = R[:, 0:1232].rearrange("p (s h k) -> p s h k", s=RING, h=HG)
        probT = R[:, 1232:3280].rearrange("p (s h q) -> p s h q", s=RING, h=HG)
        merged = R[:, 3280:3792].rearrange("p (s d) -> p s d", s=2)
        mergedT = R[:, 3792:4304].rearrange("p (s k q) -> p s k q", s=2, k=KD)
        x2T = by_chunk(R[:, 4304:5328])
        xt = R[:, 0:256]
        xtT = R[:, 256:512].rearrange("p (k q) -> p k q", k=KD)
        hb = R[:, 512:1536]
        hg = R[:, 1536:2560]
        hgT = R[:, 2560:3584].rearrange("p (k q) -> p k q", k=KF)
        yt = R[:, 3584:3840]
        b2_s = R[:, 3840:5888].rearrange("p (e d) -> p e d", e=E)
        y_of = [W1[:, c * TILES * D:(c + 1) * TILES * D].rearrange("p (t d) -> p t d", t=TILES) for c in range(TOPK)]
        acc = [W2[:, n * 1024:(n + 1) * 1024].rearrange("p (j d) -> p j d", j=CT) for n in range(2)]
        zed = W2[:, 6656:7680].rearrange("p (j d) -> p j d", j=CT)
        fin = W2[:, 2048:6144].rearrange("p (t d) -> p t d", t=TILES)
        lnw_s = W2[:, 6144:6144 + D]
        lnb_s = W2[:, 6400:6400 + D]

        ident = sb("identity", [P, P])
        mask_b = sb("mask_bias", [P, S], BF16)
        mask_raw = slot(11)[0:SC, 0:S // 4].bitcast(U8)
        eye4 = sb("identity_per_head", [P, HG, SC], BF16)
        gam = sb("gamma", [P, KD])
        bet = sb("beta", [P, KD])
        bk_s = sb("bk", [P, KD])
        bka_s = sb("bka", [P, KD])
        bv_s = sb("bv", [P, KD])
        norms = []
        for n in range(3):
            norm = {m: sb(f"ln{n}_{m}", [P, CT]) for m in ("mdiff", "msum", "vsum", "msq", "mean", "veps", "rstd")}
            norm["stats"] = sb(f"ln{n}_stats", [P, CT, 6])
            norm.update((m, sem(f"ln{n}_{m}")) for m in ("stats_done", "moments_done", "var_ready", "rstd_ready"))
            norms.append(norm)
        LN1, LN2, LN3 = norms
        carry = sb("carry", [P, CARRIES, 2, KD])
        start = sb("chunk_start", [P, 2, KD])
        mhalf = sb("minus_half", [P, CT])
        one_c = sb("one", [P, 1])
        smax = sb("score_max", [P, 2, HEADS])
        psum_r = sb("prob_sum_recip", [P, HEADS])
        pscale = sb("prob_scale", [P, HEADS])
        logits = sb("logits", [P, TILES, E])
        weight = [sb(f"choice_weight{c}", [P, TILES]) for c in range(TOPK)]
        where = [sb(f"choice_slot{c}", [P, TILES], U32) for c in range(TOPK)]
        expert_of = sb("expert_of_tile", [P, XS_TILES], I32)

        at = [0]

        def tmp(*shape):
            n = 1
            for m in shape:
                n *= m
            at[0] += n
            assert at[0] <= 3840
            v = R[:, at[0] - n:at[0]]
            if len(shape) == 2:
                v = v.rearrange("p (a b) -> p a b", a=shape[0])
            return v

        m1, m2, first = tmp(TILES), tmp(TILES), tmp(TILES)
        hot = [tmp(TILES, E) for _ in range(TOPK)]
        cand, rest = tmp(TILES, E), tmp(TILES, E)
        both = tmp(TILES, E)
        ex, den = tmp(TILES), tmp(TILES)
        tot, run = tmp(E, TILES), tmp(E, TILES)
        ones_r = tmp(E * TILES)
        starts, count, ntile, tbend, adj = tmp(E), tmp(E), tmp(E), tmp(E), tmp(E)
        counti = tmp(E)
        slots = tmp(TILES, E)
        picked = tmp(TILES, E)
        slotf = tmp(TILES)
        rev = tmp(E)
        tau = tmp(XS_TILES, E)
        tge = tmp(XS_TILES, E)
        tri = tmp(P)
        ones_m = tmp(P)
        tilef = tmp(XS_TILES)

        zero_t = X2[:, TILES - 1, :]
        hmask = slot(8)[:, 0:HC]

        pa = ctx.enter_context(nc.psum_tensor("psum_a", [P, KD, 512], F32))
        pb = ctx.enter_context(nc.psum_tensor("psum_b", [P, KD, 512], F32))
        pc = ctx.enter_context(nc.psum_tensor("psum_c", [P, KD, 512], F32))
        pv = ctx.enter_context(nc.psum_tensor("psum_v", [P, 512], F32))
        pm = ctx.enter_context(nc.psum_tensor("psum_m", [P, 512], F32))
        pb_t = pb[:, :, :].rearrange("p a (b d) -> p (a b) d", d=D)

        (consts_in, weights_in, ctx_in, experts_in, late_in, ln_in, zero_made, pads_zeroed, made, mask_made,
         ctx_mm, kv_made, x_in, x_free, h0_ready, hT_mm, hT_ready, k_mm, kT_ready, ka_mm, kexp_ready, started, key_sum,
         kk_ready, recip_ready, kw_ready, pooled_ready, v_mm, attn_ready, at_mm, x1_ready, x1_kept, x1T_mm, x1T_ready,
         q_mm, qT_ready, s_mm, max_ready, sub_ready, exp_ready, pT_mm, pT_ready, pv_mm, rec_ready, scale_ready,
         merged_ready, mT_mm, mT_ready, o_mm, r2_ready, x2_ready, x2_kept, x2T_mm, x2T_ready, lg_mm, lg_ready,
         bka_ready, carry_zero) = (sem(n) for n in (
             "consts_in weights_in ctx_in experts_in late_in ln_in zero_made pads_zeroed made mask_made "
             "ctx_mm kv_made x_in x_free h0_ready hT_mm hT_ready k_mm kT_ready ka_mm kexp_ready started key_sum "
             "kk_ready recip_ready kw_ready pooled_ready v_mm attn_ready at_mm x1_ready x1_kept x1T_mm x1T_ready "
             "q_mm qT_ready s_mm max_ready sub_ready exp_ready pT_mm pT_ready pv_mm rec_ready scale_ready "
             "merged_ready mT_mm mT_ready o_mm r2_ready x2_ready x2_kept x2T_mm x2T_ready lg_mm lg_ready "
             "bka_ready carry_zero").split())
        (route_consts, route, ex_ready, count_mm, slots_ready, scattered, table_ready, xt_in, xt_mm, xt_ready, h_mm,
         hb_ready, hg_ready, hgT_mm, hgT_ready, y_mm, y_ready, y_out, fin_step, fin_ready, fin_out,
         route_rows) = (
            sem(n) for n in (
                "route_consts route ex_ready count_mm slots_ready scattered table_ready xt_in xt_mm xt_ready h_mm "
                "hb_ready hg_ready hgT_mm hgT_ready y_mm y_ready y_out fin_step fin_ready fin_out "
                "route_rows").split())
        gathered = [sem(f"gathered{t}") for t in range(TILES)]

        block = ctx.enter_context(nc.Block())

        @block.sync
        def _(sp):
            sp.dma_start(xc, x_rows[:, 0:CT, :]).then_inc(x_in, 16)
            for dst, src in ((gam, gamma), (bet, beta), (bk_s, bk), (bka_s, bka), (bv_s, bv)):
                with nc.allow_non_contiguous_dma(reason="256 values, one per partition"):
                    sp.dma_start(dst[:, :], src.rearrange("(k p) -> p k", p=P)).then_inc(consts_in, 16)
            for dst, src in ((wk_s, wk), (wka_s, wka), (wv_s, wv)):
                sp.dma_start(dst, src.rearrange("(k p) n -> p k n", p=P)).then_inc(weights_in, 16)
            sp.dma_start(ctx_s, ctxT.rearrange("(k p) n -> p k n", p=P)).then_inc(ctx_in, 16)
            sp.dma_start(mask_raw, maskT).then_inc(ctx_in, 16)
            for dst, src in ((wxk_s, wxk), (wxv_s, wxv), (wq_s, wq), (wo_s, wo)):
                sp.dma_start(dst, src.rearrange("(k p) n -> p k n", p=P)).then_inc(ctx_in, 16)
            sp.dma_start(rw_s, rw.rearrange("(k p) e -> p k e", p=P)).then_inc(ctx_in, 16)
            sp.dma_start(rb_s, rb.partition_broadcast(P)).then_inc(ctx_in, 16)
            sp.wait_ge(zero_made, 1)
            sp.dma_start(xs_tiles, zero_t.rearrange("p (a d) -> p a d", a=1).to_broadcast([P, XS_TILES, D])).then_inc(pads_zeroed, 16)
            for e in range(EARLY):
                sp.dma_start(w1_v[:, e], w1[e].rearrange("(k p) f -> p k f", p=P)).then_inc(experts_in, 16)
                sp.dma_start(w2_v[:, e], w2[e].rearrange("(k p) d -> p k d", p=P)).then_inc(experts_in, 16)
            with sp.Fori(0, CHUNKS - 1) as it:
                sp.wait_ge(x_free, it + 1)
                sp.dma_start(xc, x_rows[:, bass.ds(it * CT + CT, CT), :]).then_inc(x_in, 16)
            sp.wait_ge(lg_ready, CHUNKS)
            sp.wait_ge(x2_kept, CHUNKS)
            for e in range(EARLY, E):
                sp.dma_start(w1_v[:, e], w1[e].rearrange("(k p) f -> p k f", p=P)).then_inc(experts_in, 16)
                sp.dma_start(w2_v[:, e], w2[e].rearrange("(k p) d -> p k d", p=P)).then_inc(experts_in, 16)
            sp.dma_start(LATE[:, :], b1.rearrange("e f -> (e f)").partition_broadcast(P)).then_inc(late_in, 16)
            sp.dma_start(R[:, 3840:5888], b2.rearrange("e d -> (e d)").partition_broadcast(P)).then_inc(late_in, 16)

            sp.wait_ge(scattered, TOPK * TILES * 16)
            sp.wait_ge(route, ROUTE_STEPS)
            sp.dma_start(xt, xs_tiles[:, 0, :]).then_inc(xt_in, 16)
            sp.wait_ge(xt_mm, 1)
            sp.dma_start(xt, xs_tiles[:, 1, :]).then_inc(xt_in, 16)
            with sp.Fori(1, SLOT_TILES) as t:
                sp.wait_ge(xt_mm, t + 1)
                sp.dma_start(xt, xs_tiles[:, bass.ds(t + 1, 1), :]).then_inc(xt_in, 16)
                sp.wait_ge(y_ready, t)
                sp.dma_start(ys_tiles[:, bass.ds(t - 1, 1), :], yt).then_inc(y_out, 16)
            sp.wait_ge(y_ready, SLOT_TILES)
            sp.dma_start(ys_tiles[:, SLOT_TILES - 1, :], yt).then_inc(y_out, 16)
            sp.dma_start(lnw_s, lnw.partition_broadcast(P)).then_inc(ln_in, 16)
            sp.dma_start(lnb_s, lnb.partition_broadcast(P)).then_inc(ln_in, 16)
            for g in range(TILES // CT):
                sp.wait_ge(fin_ready, g + 1)
                sp.dma_start(out_rows[:, g * CT:(g + 1) * CT, :], fin[:, g * CT:(g + 1) * CT, :]).then_inc(fin_out, 16)
            sp.wait_ge(fin_out, 16 * (TILES // CT))
            sp.wait_ge(xt_in, 16 * XS_TILES)

        @block.gpsimd
        def _(pool):
            pool.memset(zero_t, 0.0).then_inc(zero_made, 1)
            pool.memset(mhalf[:, :], -0.5).then_inc(made, 1)
            pool.memset(ident[:, :], 0.0).then_inc(made, 1)
            pool.memset(eye4[:, :, :], 0.0).then_inc(made, 1)
            pool.memset(hmask, 1.0).then_inc(made, 1)
            pool.memset(one_c[:, :], 1.0).then_inc(made, 1)
            pool.wait_ge(made, 5)
            pool.affine_select(out=ident[:, :], in_=ident[:, :], compare_op=ALU.not_equal, fill=1.0, base=0,
                               pattern=[[-1, P]], channel_multiplier=1).then_inc(made, 1)
            pool.affine_select(out=eye4[:, :, :], in_=eye4[:, :, :], compare_op=ALU.not_equal, fill=1.0, base=0,
                               pattern=[[0, HG], [-1, SC]], channel_multiplier=1).then_inc(made, 1)
            pool.affine_select(out=hmask, in_=hmask, compare_op=ALU.is_ge, fill=0.0, base=0,
                               pattern=[[-DK, HC]], channel_multiplier=1).then_inc(made, 1)
            pool.wait_ge(made, 8)
            pool.affine_select(out=hmask, in_=hmask, compare_op=ALU.is_ge, fill=0.0, base=DK - 1,
                               pattern=[[DK, HC]], channel_multiplier=-1).then_inc(made, 1)

            def rsqrt(norm, count):
                pool.wait_ge(norm["var_ready"], count)
                pool.tensor_tensor(norm["rstd"][:, :], norm["veps"][:, :], mhalf[:, :], ALU.pow).then_inc(norm["rstd_ready"], 1)

            def output(it):
                rsqrt(LN3, it + 1)
                pool.wait_ge(x2_ready, it + 1)
                pool.tensor_copy(X2[:, bass.ds(it * CT, CT), :], x2c).then_inc(x2_kept, 1)

            def self_attention(n, prev=None):
                rsqrt(LN1, n + 1)
                if prev is not None:
                    output(prev)
                pool.wait_ge(key_sum, n + 1)
                pool.tensor_tensor(kexp, kexp, keysT, ALU.mult).then_inc(kk_ready, 1)
                rsqrt(LN2, n + 1)
                pool.wait_ge(x1_ready, n + 1)
                pool.tensor_copy(X2[:, bass.ds(n * CT, CT), :], x1).then_inc(x1_kept, 1)

            pool.wait_ge(pads_zeroed, 16)
            self_attention(0)
            self_attention(1)
            with pool.Fori(1, CHUNKS - 1) as it:
                self_attention(it + 1, it - 1)
            output(CHUNKS - 2)
            output(CHUNKS - 1)

            pool.wait_ge(lg_ready, CHUNKS)
            pool.iota(tau, pattern=[[1, XS_TILES], [0, E]], base=0, channel_multiplier=0,
                      allow_small_or_imprecise_dtypes=True).then_inc(route_consts, 1)
            pool.iota(rev, pattern=[[-1, E]], base=E, channel_multiplier=0,
                      allow_small_or_imprecise_dtypes=True).then_inc(route_consts, 1)
            pool.memset(ones_m, 1.0).then_inc(route_consts, 1)
            pool.memset(ones_r, 1.0).then_inc(route_consts, 1)
            pool.wait_ge(route_consts, 4)
            pool.affine_select(out=tri, in_=ones_m, compare_op=ALU.is_gt, fill=0.0, base=0,
                               pattern=[[1, P]], channel_multiplier=-1).then_inc(route_consts, 1)

            pool.wait_ge(pads_zeroed, 16)
            pool.wait_ge(slots_ready, TOPK)
            for t in range(TILES):
                for c in range(TOPK):
                    pool.indirect_dma_start(xs, bass.IndirectOffsetOnAxis(where[c][:, t:t + 1], 0), X2[:, t, :],
                                            None).then_inc(scattered, 16)
            pool.wait_ge(y_out, 16 * SLOT_TILES)
            def gather(g):
                for t in range(g * CT, g * CT + CT):
                    for c in range(TOPK):
                        pool.indirect_dma_start(y_of[c][:, t, :], None, ys,
                                                bass.IndirectOffsetOnAxis(where[c][:, t:t + 1], 0)).then_inc(gathered[t], 16)

            for g in range(GROUPS + 2):
                if g < GROUPS:
                    gather(g)
                if 1 <= g <= GROUPS:
                    rsqrt(LN1, CHUNKS + g)
                if g >= 2:
                    rsqrt(LN2, CHUNKS + g - 1)

        @block.scalar
        def _(act):
            act.wait_ge(consts_in, 5 * 16)
            act.mul(bka_s[:, :], bka_s[:, :], D ** -0.5).then_inc(bka_ready, 1)
            act.wait_ge(bka_ready, 1)

            def normalised(n):
                act.wait_ge(hT_mm, n + 1)
                for k in range(KD):
                    last = act.activation(hT[:, k, :], pb[:, k, :], ACT.Identity, scale=gam[:, k:k + 1],
                                          bias=bet[:, k:k + 1])
                last.then_inc(hT_ready, 1)

            def keys(n):
                act.wait_ge(k_mm, n + 1)
                for k in range(KD):
                    last = act.activation(keysT[:, k, :], pb[:, k, :], ACT.Identity, bias=bk_s[:, k:k + 1])
                last.then_inc(kT_ready, 1)

            def key_weights(n):
                act.wait_ge(ka_mm, n + 1)
                for k in range(KD):
                    last = act.activation(kexp[:, k, :], pb[:, k, :], ACT.Exp, scale=D ** -0.5, bias=bka_s[:, k:k + 1])
                last.then_inc(kexp_ready, 1)

            def x1_features(n):
                act.wait_ge(x1T_mm, n + 1)
                act.activation(x1T, pb[:, :, :], ACT.Copy).then_inc(x1T_ready, 1)

            def queries(n):
                act.wait_ge(q_mm, n + 1)
                act.activation(qT, pb[:, :, :], ACT.Copy).then_inc(qT_ready, 1)

            def output_features(it):
                act.wait_ge(x2T_mm, it + 1)
                act.activation(x2T, pb[:, :, :], ACT.Copy).then_inc(x2T_ready, 1)

            def cross_attention(it, nxt, prev):
                def turned_probs(h):
                    act.wait_ge(pT_mm, it * STEPS + h + 1)
                    act.activation(probT[0:SC, h % RING], pc[0:SC, h % 2, :].rearrange("p (h q) -> p h q", h=HG),
                                   ACT.Copy).then_inc(pT_ready, 1)

                def turned_heads(j):
                    act.wait_ge(mT_mm, it * CT + j + 1)
                    act.activation(mergedT[:, j % 2], pm[:, 0:D].rearrange("p (k q) -> p k q", k=KD),
                                   ACT.Copy).then_inc(mT_ready, 1)

                for h in range(STEPS):
                    act.wait_ge(sub_ready, it * STEPS + h + 1)
                    act.activation(prob[:, h % RING], prob[:, h % RING], ACT.Exp, scale=DK ** -0.5).then_inc(exp_ready, 1)
                    if h >= 1:
                        turned_probs(h - 1)
                    if h >= QUADS and h % QUADS == 2:
                        turned_heads(h // QUADS - 1)
                    if nxt is not None:
                        if h == 3:
                            normalised(nxt)
                        if h == 4:
                            keys(nxt)
                        if h == 5:
                            key_weights(nxt)
                        if h == 15:
                            x1_features(nxt)
                    if prev is not None and h == 7:
                        output_features(prev)
                turned_probs(STEPS - 1)
                turned_heads(CT - 1)
                if nxt is not None:
                    queries(nxt)

            for stage in (normalised, keys, key_weights, x1_features, queries):
                stage(0)
            cross_attention(0, 1, None)
            with act.Fori(1, CHUNKS - 1) as it:
                cross_attention(it, it + 1, it - 1)
            cross_attention(CHUNKS - 1, None, CHUNKS - 2)
            output_features(CHUNKS - 1)

            act.wait_ge(route, ROUTE_DIFF)
            act.activation(ex, ex, ACT.Exp).then_inc(ex_ready, 1)

            with act.Fori(0, SLOT_TILES) as t:
                for n in range(2):
                    act.wait_ge(hb_ready, t * 2 + n + 1)
                    act.activation(hg[:, n * 512:(n + 1) * 512], hb[:, n * 512:(n + 1) * 512],
                                   ACT.Gelu).then_inc(hg_ready, 1)
                act.wait_ge(hgT_mm, t * 2 + 1)
                act.activation(hgT[:, 0:KF // 2, :], pb[:, 0, :].rearrange("p (k q) -> p k q", k=KF // 2),
                               ACT.Copy).then_inc(hgT_ready, 1)

        @block.vector
        def _(dve):
            def moments(norm, src, eps, count):
                stats = norm["stats"]
                for j in range(CT):
                    last = dve.bn_stats(stats[:, j, :], src[:, j, :])
                last.then_inc(norm["stats_done"], 1)
                mean_e, mean_o, var_e, var_o = stats[:, :, 1], stats[:, :, 4], stats[:, :, 2], stats[:, :, 5]
                dve.wait_ge(norm["stats_done"], count)
                dve.tensor_tensor(norm["mdiff"][:, :], mean_e, mean_o, ALU.subtract)
                dve.tensor_tensor(norm["msum"][:, :], mean_e, mean_o, ALU.add)
                dve.scalar_tensor_tensor(norm["vsum"][:, :], var_e, D * eps, var_o, ALU.add,
                                         ALU.add).then_inc(norm["moments_done"], 1)
                dve.wait_ge(norm["moments_done"], 2 * count - 1)
                dve.scalar_tensor_tensor(norm["msq"][:, :], norm["mdiff"][:, :], 0.25, norm["mdiff"][:, :], ALU.mult, ALU.mult)
                dve.tensor_scalar(norm["mean"][:, :], norm["msum"][:, :], 0.5, None, ALU.mult).then_inc(norm["moments_done"], 1)
                dve.wait_ge(norm["moments_done"], 2 * count)
                dve.scalar_tensor_tensor(norm["veps"][:, :], norm["vsum"][:, :], 1.0 / D, norm["msq"][:, :], ALU.mult,
                                         ALU.add).then_inc(norm["var_ready"], 1)

            def normalise(norm, src, dst, count, done):
                dve.wait_ge(norm["rstd_ready"], count)
                for j in range(CT):
                    last = dve.tensor_scalar(dst[:, j, :], src[:, j, :], norm["mean"][:, j:j + 1], norm["rstd"][:, j:j + 1],
                                             ALU.subtract, ALU.mult)
                last.then_inc(done, 1)

            dve.wait_ge(ctx_in, 8 * 16)
            dve.tensor_scalar(mask_b[0:SC, :], mask_raw, MASKED, None, ALU.mult).then_inc(mask_made, 1)
            dve.memset(vaug[0:SC], 1.0).then_inc(mask_made, 1)
            dve.wait_ge(made, MADE)
            dve.wait_ge(mask_made, 2)
            dve.wait_ge(ctx_mm, 1)
            for c in range(KD):
                for b in range(B):
                    keys = pa[:, c, b * SC:(b + 1) * SC].rearrange("p (h k) -> p h k", h=1).to_broadcast([P, HC, SC])
                    dve.tensor_tensor(kbd[:, b, c], keys, hmask.rearrange("p (h k) -> p h k", k=1).to_broadcast([P, HC, SC]),
                                      ALU.mult)
            for b in range(B):
                last = dve.tensor_copy(vaug[0:SC, b, :, 0:DK], pb[0:SC, b, 0:D].rearrange("p (h v) -> p h v", h=HEADS))
            last.then_inc(kv_made, 1)

            one_s = one_c[:, 0:1].to_broadcast([P, CHUNK])
            dve.memset(carry[:, :, :, :], 0.0).then_inc(carry_zero, 1)
            dve.wait_ge(carry_zero, 1)

            def kept_in(n):
                return bass.ds(n + 1 + (n % CPB) * CHUNKS, 1)

            def input_moments(n):
                dve.wait_ge(x_in, n * 16 + 16)
                moments(LN1, xc, EPS, n + 1)

            def input_normalise(n):
                normalise(LN1, xc, h0, n + 1, h0_ready)

            def sum_weights(n):
                dve.tensor_copy(start[:, :, :], carry[:, bass.ds(n, 1)].rearrange("p a s k -> p (a s) k")).then_inc(started, 1)
                dve.wait_ge(kexp_ready, n + 1)
                dve.wait_ge(started, n + 1)
                for k in range(KD):
                    last = dve.tensor_tensor_scan(csum[:, k, :], one_s, kexp[:, k, :], start[:, 0, k:k + 1], ALU.mult, ALU.add)
                last.then_inc(key_sum, 1)
                dve.wait_ge(key_sum, n + 1)

            def invert(n, part):
                cols = slice(part % 2 * CHUNK // 2, (part % 2 + 1) * CHUNK // 2)
                dve.reciprocal(kw[:, part // 2, cols], csum[:, part // 2, cols]).then_inc(recip_ready, 1)

            def weigh_keys(n):
                dve.wait_ge(recip_ready, n * 4 + 4)
                dve.wait_ge(kk_ready, n + 1)
                dve.tensor_tensor(kw, kw, kexp, ALU.mult).then_inc(kw_ready, 1)

            def pool_keys(n):
                dve.wait_ge(kw_ready, n + 1)
                for k in range(KD):
                    last = dve.tensor_tensor_scan(pooled[:, k, :], one_s, kw[:, k, :], start[:, 1, k:k + 1], ALU.mult, ALU.add)
                last.then_inc(pooled_ready, 1)
                dve.wait_ge(pooled_ready, n + 1)
                dve.tensor_copy(carry[:, kept_in(n), 0].rearrange("p a k -> p (a k)"), csum[:, :, CHUNK - 1])
                dve.tensor_copy(carry[:, kept_in(n), 1].rearrange("p a k -> p (a k)"), pooled[:, :, CHUNK - 1])

            def times_values(n):
                dve.wait_ge(v_mm, n + 1)
                for k in range(KD):
                    last = dve.scalar_tensor_tensor(attnT[:, k, :], pb[:, k, :], bv_s[:, k:k + 1], pooled[:, k, :],
                                                    ALU.add, ALU.mult)
                last.then_inc(attn_ready, 1)

            def x1_moments(n):
                dve.wait_ge(at_mm, n + 1)
                dve.tensor_tensor(h0, pb_t, xc, ALU.add).then_inc(x_free, 1)
                dve.wait_ge(x_free, n + 1)
                moments(LN2, h0, EPS, n + 1)

            def x1_normalise(n):
                normalise(LN2, h0, x1, n + 1, x1_ready)

            def output_moments(it):
                dve.wait_ge(r2_ready, it * CT + CT)
                moments(LN3, r2, EPS, it + 1)

            def output_normalise(it):
                normalise(LN3, r2, x2c, it + 1, x2_ready)

            def route_logits(it):
                dve.wait_ge(lg_mm, it + 1)
                dve.wait_ge(x2_kept, it + 1)
                dve.tensor_tensor(logits[:, bass.ds(it * CT, CT), :], pb[:, 0, 0:CT * E].rearrange("p (j e) -> p j e", j=CT),
                                  rb_s.rearrange("p (j e) -> p j e", j=1).to_broadcast([P, CT, E]),
                                  ALU.add).then_inc(lg_ready, 1)

            def cross_attention(it, nxt, prev):
                def residual(j):
                    dve.wait_ge(x1_kept, it + 1)
                    dve.wait_ge(o_mm, it * CT + j + 1)
                    dve.tensor_tensor(r2[:, j, :], pm[:, D:2 * D], X2[:, bass.ds(it * CT + j, 1), :].rearrange("p a d -> p (a d)"),
                                      ALU.add).then_inc(r2_ready, 1)

                def normalise_heads(j):
                    dve.wait_ge(pv_mm, it * CT + j + 1)
                    sums = pv[:, 0:HEADS * VW].rearrange("p (h v) -> p h v", h=HEADS)
                    dve.reciprocal(psum_r[:, :], sums[:, :, DK]).then_inc(rec_ready, 1)
                    dve.wait_ge(rec_ready, it * CT + j + 1)
                    dve.scalar_tensor_tensor(pscale[:, :], smax[:, j % 2, :], MASKED / 10, psum_r[:, :], ALU.is_gt,
                                             ALU.mult).then_inc(scale_ready, 1)
                    dve.wait_ge(scale_ready, it * CT + j + 1)
                    dve.tensor_tensor(merged[:, j % 2, :].rearrange("p (h v) -> p h v", h=HEADS), sums[:, :, 0:DK],
                                      pscale[:, :].rearrange("p (h v) -> p h v", v=1).to_broadcast([P, HEADS, DK]),
                                      ALU.mult).then_inc(merged_ready, 1)

                for h in range(STEPS):
                    j, quad = divmod(h, QUADS)
                    scores = pa[:, h % 2, 0:HG * SC].rearrange("p (h k) -> p h k", h=HG)
                    top = smax[:, j % 2, quad * HG:(quad + 1) * HG]
                    dve.wait_ge(s_mm, it * STEPS + h + 1)
                    dve.tensor_reduce(top, scores, AX.X, ALU.max).then_inc(max_ready, 1)
                    dve.wait_ge(max_ready, it * STEPS + h + 1)
                    dve.tensor_tensor(prob[:, h % RING], scores,
                                      top.rearrange("p (h k) -> p h k", k=1).to_broadcast([P, HG, SC]),
                                      ALU.subtract).then_inc(sub_ready, 1)
                    if h >= QUADS and quad == 1:
                        normalise_heads(j - 1)
                    if h >= QUADS and quad == QUADS - 1:
                        residual(j - 1)
                    if nxt is not None:
                        if h == 1:
                            input_moments(nxt)
                        if h == 2:
                            input_normalise(nxt)
                        if h == 6:
                            sum_weights(nxt)
                        if h in (7, 8, 9, 10):
                            invert(nxt, h - 7)
                        if h == 10:
                            weigh_keys(nxt)
                        if h == 11:
                            pool_keys(nxt)
                        if h == 12:
                            times_values(nxt)
                        if h == 13:
                            x1_moments(nxt)
                        if h == 14:
                            x1_normalise(nxt)
                    if prev is not None:
                        if h == 3:
                            output_moments(prev)
                        if h == 4:
                            output_normalise(prev)
                        if h == 8:
                            route_logits(prev)
                normalise_heads(CT - 1)
                residual(CT - 1)

            input_moments(0)
            input_normalise(0)
            sum_weights(0)
            for part in range(4):
                invert(0, part)
            for stage in (weigh_keys, pool_keys, times_values, x1_moments, x1_normalise):
                stage(0)
            cross_attention(0, 1, None)
            with dve.Fori(1, CHUNKS - 1) as it:
                cross_attention(it, it + 1, it - 1)
            cross_attention(CHUNKS - 1, None, CHUNKS - 2)
            output_moments(CHUNKS - 1)
            output_normalise(CHUNKS - 1)
            route_logits(CHUNKS - 1)

            steps = [0]

            def then(ins):
                steps[0] += 1
                ins.then_inc(route, 1)
                dve.wait_ge(route, steps[0])

            def per_e(ap):
                return ap.rearrange("p (a e) -> p a e", a=1).to_broadcast([P, TILES, E])

            def per_t(ap):
                return ap.rearrange("p (t e) -> p t e", e=1).to_broadcast([P, TILES, E])

            dve.wait_ge(lg_ready, CHUNKS)
            dve.wait_ge(route_consts, 5)
            lg = logits[:, :, :]
            for c, (src, top) in enumerate(((lg, m1), (rest, m2))):
                then(dve.tensor_reduce(top, src, AX.X, ALU.max))
                then(dve.tensor_tensor(cand, src, per_t(top), ALU.is_equal))
                then(dve.tensor_tensor(cand, cand, per_e(rev), ALU.mult))
                then(dve.tensor_reduce(first, cand, AX.X, ALU.max))
                then(dve.tensor_tensor(hot[c], cand, per_t(first), ALU.is_equal))
                if c == 0:
                    then(dve.scalar_tensor_tensor(rest, hot[0], -3e38, lg, ALU.mult, ALU.add))
            then(dve.tensor_tensor(both, hot[0], hot[1], ALU.add))
            assert steps[0] == ROUTE_BOTH
            then(dve.tensor_tensor(ex, m2, m1, ALU.subtract))
            assert steps[0] == ROUTE_DIFF
            dve.wait_ge(count_mm, 1)
            then(dve.tensor_copy(tot, pv[:, P:2 * P].rearrange("p (t e) -> p e t", e=E)))
            then(dve.tensor_tensor_scan(run.rearrange("p e t -> p (e t)"), ones_r, tot.rearrange("p e t -> p (e t)"), 0.0,
                                        ALU.mult, ALU.add))
            then(dve.memset(starts[:, 0:1], 0.0))
            then(dve.tensor_copy(starts[:, 1:E], run[:, 0:E - 1, TILES - 1]))
            then(dve.tensor_tensor(count, run[:, :, TILES - 1], starts, ALU.subtract))
            then(dve.tensor_scalar(counti.bitcast(I32), count, float(P - 1), None, ALU.add))
            then(dve.tensor_scalar(counti.bitcast(I32), counti.bitcast(I32), 7, None, ALU.logical_shift_right))
            then(dve.tensor_copy(ntile, counti.bitcast(I32)))
            then(dve.tensor_tensor_scan(tbend, ones_r[:, 0:E], ntile, 0.0, ALU.mult, ALU.add))
            then(dve.tensor_tensor(adj, tbend, ntile, ALU.subtract))
            then(dve.scalar_tensor_tensor(adj, adj, float(P), starts, ALU.mult, ALU.subtract))
            then(dve.tensor_tensor(run, run, tot, ALU.subtract))
            then(dve.tensor_tensor(run, run, adj.rearrange("p (e t) -> p e t", t=1).to_broadcast([P, E, TILES]), ALU.add))
            then(dve.tensor_tensor(slots, pv[:, 0:P].rearrange("p (t e) -> p t e", e=E),
                                   run.rearrange("p e t -> p t e"), ALU.add))
            for c in range(TOPK):
                then(dve.tensor_tensor(picked, slots, hot[c], ALU.mult))
                then(dve.tensor_reduce(slotf, picked, AX.X, ALU.add))
                dve.tensor_copy(where[c][:, :], slotf).then_inc(slots_ready, 1)
            dve.wait_ge(slots_ready, TOPK)
            then(dve.tensor_tensor(tge, tau, tbend.rearrange("p (t e) -> p t e", t=1).to_broadcast([P, XS_TILES, E]),
                                   ALU.is_ge))
            then(dve.tensor_reduce(tilef, tge, AX.X, ALU.add))
            dve.tensor_scalar(expert_of[:, :], tilef, float(E - 1), None, ALU.min).then_inc(table_ready, 1)
            dve.wait_ge(table_ready, 1)
            dve.wait_ge(ex_ready, 1)
            then(dve.tensor_scalar(den, ex, 1.0, None, ALU.add))
            then(dve.reciprocal(weight[0][:, :], den))
            then(dve.tensor_tensor(weight[1][:, :], weight[0][:, :], ex, ALU.mult))
            assert steps[0] == ROUTE_STEPS

            dve.wait_ge(late_in, 2 * 16)

            def copy_xtT(n):
                dve.wait_ge(xt_mm, n)
                dve.tensor_copy(xtT, pm[:, 0:D].rearrange("p (k q) -> p k q", k=KD)).then_inc(xt_ready, 1)

            def hidden(t, e):
                for n in range(2):
                    dve.wait_ge(h_mm, t * 2 + n + 1)
                    dve.tensor_tensor(hb[:, n * 512:(n + 1) * 512], pa[:, n, :],
                                      b1_s[:, bass.ds(e, 1), n * 512:(n + 1) * 512].rearrange("p a f -> p (a f)"),
                                      ALU.add).then_inc(hb_ready, 1)
                copy_xtT(t + 2)

            def copy_hgT(t):
                dve.wait_ge(hgT_mm, t * 2 + 2)
                dve.tensor_copy(hgT[:, KF // 2:KF, :],
                                pb[:, 1, :].rearrange("p (k q) -> p k q", k=KF // 2)).then_inc(hgT_ready, 1)

            def finish_tile(n, e):
                dve.wait_ge(y_mm, n)
                dve.tensor_tensor(yt, pv[:, 0:D], b2_s[:, bass.ds(e, 1), :].rearrange("p a d -> p (a d)"),
                                  ALU.add).then_inc(y_ready, 1)

            def expert(t):
                return nc.values_load(expert_of[0:1, bass.ds(t, 1)], engines=[mybir.EngineType.DVE], min_val=0, max_val=E - 1,
                                      skip_runtime_bounds_check_because="the table is clamped to the experts")

            copy_xtT(1)
            hidden(0, expert(0))
            copy_hgT(0)
            with dve.Fori(1, SLOT_TILES) as t:
                e_before = expert(t - 1)
                hidden(t, expert(t))
                finish_tile(t, e_before)
                copy_hgT(t)
                dve.wait_ge(y_out, t * 16)
            finish_tile(SLOT_TILES, expert(SLOT_TILES - 1))

            dve.wait_ge(ln_in, 2 * 16)
            fs = [0]

            def step(ins):
                fs[0] += 1
                ins.then_inc(fin_step, 1)
                dve.wait_ge(fin_step, fs[0])

            def combine(g):
                for j in range(CT):
                    t = g * CT + j
                    dve.wait_ge(gathered[t], TOPK * 16)
                    last = dve.scalar_tensor_tensor(acc[g % 2][:, j, :], y_of[0][:, t, :], weight[0][:, t:t + 1], X2[:, t, :],
                                                    ALU.mult, ALU.add)
                step(last)
                for j in range(CT):
                    t = g * CT + j
                    last = dve.scalar_tensor_tensor(acc[g % 2][:, j, :], y_of[1][:, t, :], weight[1][:, t:t + 1],
                                                    acc[g % 2][:, j, :], ALU.mult, ALU.add)
                step(last)
                moments(LN1, acc[g % 2], EPS_FFN, CHUNKS + g + 1)

            def scale_and_add(g):
                dve.wait_ge(LN1["rstd_ready"], CHUNKS + g + 1)
                for j in range(CT):
                    last = dve.scalar_tensor_tensor(zed[:, j, :], acc[g % 2][:, j, :], LN1["mean"][:, j:j + 1], lnw_s,
                                                    ALU.subtract, ALU.mult)
                step(dve.tensor_tensor(fin[:, g * CT:(g + 1) * CT, :], X2[:, g * CT:(g + 1) * CT, :],
                                       lnb_s.rearrange("p (j d) -> p j d", j=1).to_broadcast([P, CT, D]), ALU.add))
                for j in range(CT):
                    last = dve.scalar_tensor_tensor(fin[:, g * CT + j, :], zed[:, j, :], LN1["rstd"][:, j:j + 1],
                                                    fin[:, g * CT + j, :], ALU.mult, ALU.add)
                step(last)
                moments(LN2, fin[:, g * CT:(g + 1) * CT, :], EPS, CHUNKS + g + 1)

            def finish(g):
                rows = fin[:, g * CT:(g + 1) * CT, :]
                normalise(LN2, rows, rows, CHUNKS + g + 1, fin_ready)

            combine(0)
            for g in range(GROUPS):
                scale_and_add(g)
                if g + 1 < GROUPS:
                    combine(g + 1)
                finish(g)

        @block.tensor
        def _(pe):
            pe.wait_ge(ctx_in, 8 * 16)
            for c in range(KD):
                for k in range(KD):
                    pe.matmul(pa[:, c, 0:B * SC], wxk_s[:, k, c * P:(c + 1) * P], ctx_s[:, k, :], start=(k == 0),
                              stop=(k == KD - 1))
            for b in range(B):
                for k in range(KD):
                    last = pe.matmul(pb[0:SC, b, 0:D], ctx_s[:, k, b * SC:(b + 1) * SC], wxv_s[:, k, :], start=(k == 0),
                                     stop=(k == KD - 1))
            last.then_inc(ctx_mm, 1)
            pe.wait_ge(weights_in, 3 * 16)
            pe.wait_ge(made, MADE)
            pe.wait_ge(kv_made, 1)

            def project(dst, w, src):
                for c in range(KD):
                    for k in range(KD):
                        last = pe.matmul(dst[:, c, :], w[:, k, c * P:(c + 1) * P], src[:, k, :], start=(k == 0),
                                         stop=(k == KD - 1))
                return last

            def to_features(dst, src):
                for j in range(CT):
                    for k in range(KD):
                        last = pe.transpose(dst[:, k, j * P:(j + 1) * P], src[:, j, k * P:(k + 1) * P], ident[:, :])
                return last

            def normalised(n):
                pe.wait_ge(h0_ready, n + 1)
                to_features(pb, h0).then_inc(hT_mm, 1)

            def keys(n):
                pe.wait_ge(hT_ready, n + 1)
                project(pb, wk_s, hT).then_inc(k_mm, 1)

            def key_weights(n):
                pe.wait_ge(kT_ready, n + 1)
                project(pb, wka_s, keysT).then_inc(ka_mm, 1)

            def values(n, prev=None):
                pe.wait_ge(kexp_ready, n + 1)
                if prev is not None:
                    pe.wait_ge(lg_ready, prev + 1)
                project(pb, wv_s, hT).then_inc(v_mm, 1)

            def turn_attention(n):
                pe.wait_ge(attn_ready, n + 1)
                for j in range(CT):
                    for k in range(KD):
                        last = pe.transpose(pb_t[:, j, k * P:(k + 1) * P], attnT[:, k, j * P:(j + 1) * P], ident[:, :])
                last.then_inc(at_mm, 1)

            def x1_features(n):
                pe.wait_ge(x1_ready, n + 1)
                to_features(pb, x1).then_inc(x1T_mm, 1)

            def queries(n):
                pe.wait_ge(x1T_ready, n + 1)
                project(pb, wq_s, x1T).then_inc(q_mm, 1)

            def output_features(it):
                pe.wait_ge(x2_ready, it + 1)
                to_features(pb, x2c).then_inc(x2T_mm, 1)

            def route_logits(it):
                pe.wait_ge(x2T_ready, it + 1)
                for j in range(CT):
                    for k in range(KD):
                        last = pe.matmul(pb[:, 0, j * E:(j + 1) * E], x2T[:, k, j * P:(j + 1) * P], rw_s[:, k, :],
                                         start=(k == 0), stop=(k == KD - 1))
                last.then_inc(lg_mm, 1)

            def cross_attention(it, nxt, prev):
                b = it // CPB

                def scores(h):
                    j, quad = divmod(h, QUADS)
                    half, g = divmod(quad, HC // HG)
                    if h >= 2:
                        pe.wait_ge(sub_ready, it * STEPS + h - 1)
                    dst = pa[:, h % 2, 0:HG * SC]
                    pe.matmul(dst, qT[:, half, j * P:(j + 1) * P],
                              kbd[:, bass.ds(b, 1), half, g * HG:(g + 1) * HG, :].rearrange("p a h k -> p (a h k)"),
                              start=True, stop=False)
                    pe.matmul(dst, mask_b[0:SC, bass.ds((it % CPB) * CHUNK + j * P, P)],
                              eye4[0:SC, :, :].rearrange("p h k -> p (h k)"), start=False, stop=True).then_inc(s_mm, 1)

                def turn_probs(h):
                    pe.wait_ge(exp_ready, it * STEPS + h + 1)
                    if h >= 2:
                        pe.wait_ge(pT_ready, it * STEPS + h - 1)
                    for n in range(HG):
                        last = pe.transpose(pc[0:SC, h % 2, n * P:(n + 1) * P], prob[:, h % RING, n, :], ident[:, :])
                    last.then_inc(pT_mm, 1)

                def weigh_values(h):
                    j, quad = divmod(h, QUADS)
                    pe.wait_ge(pT_ready, it * STEPS + h + 1)
                    if quad == 0 and j >= 1:
                        pe.wait_ge(merged_ready, it * CT + j)
                    for n in range(HG):
                        head = quad * HG + n
                        last = pe.matmul(pv[:, head * VW:(head + 1) * VW], probT[0:SC, h % RING, n, :],
                                         vaug[0:SC, bass.ds(b, 1), head, :].rearrange("p a v -> p (a v)"),
                                         start=True, stop=True)
                    if quad == QUADS - 1:
                        last.then_inc(pv_mm, 1)

                def turn_heads(j):
                    pe.wait_ge(merged_ready, it * CT + j + 1)
                    for k in range(KD):
                        last = pe.transpose(pm[:, k * P:(k + 1) * P], merged[:, j % 2, k * P:(k + 1) * P], ident[:, :])
                    last.then_inc(mT_mm, 1)

                def project_out(j):
                    pe.wait_ge(mT_ready, it * CT + j + 1)
                    if j >= 1:
                        pe.wait_ge(r2_ready, it * CT + j)
                    for k in range(KD):
                        last = pe.matmul(pm[:, D:2 * D], mergedT[:, j % 2, k, :], wo_s[:, k, :], start=(k == 0),
                                         stop=(k == KD - 1))
                    last.then_inc(o_mm, 1)

                pe.wait_ge(qT_ready, it + 1)
                scores(0)
                scores(1)
                turn_probs(0)
                for h in range(STEPS):
                    if h + 2 < STEPS:
                        scores(h + 2)
                    if h + 1 < STEPS:
                        turn_probs(h + 1)
                    weigh_values(h)
                    if h >= QUADS and h % QUADS == 0:
                        turn_heads(h // QUADS - 1)
                    if h >= QUADS and h % QUADS == 1:
                        project_out(h // QUADS - 1)
                    if nxt is not None:
                        if h == 1:
                            normalised(nxt)
                        if h == 2:
                            keys(nxt)
                        if h == 3:
                            key_weights(nxt)
                    if prev is not None:
                        if h == 5:
                            output_features(prev)
                        if h == 6:
                            route_logits(prev)
                    if nxt is not None:
                        if h == 8:
                            values(nxt, prev)
                        if h == 11:
                            turn_attention(nxt)
                        if h == 13:
                            x1_features(nxt)
                turn_heads(CT - 1)
                if nxt is not None:
                    queries(nxt)
                project_out(CT - 1)

            for stage in (normalised, keys, key_weights, values, turn_attention, x1_features, queries):
                stage(0)
            cross_attention(0, 1, None)
            with pe.Fori(1, CHUNKS - 1) as it:
                cross_attention(it, it + 1, it - 1)
            cross_attention(CHUNKS - 1, None, CHUNKS - 2)
            output_features(CHUNKS - 1)
            route_logits(CHUNKS - 1)

            pe.wait_ge(route_consts, 5)
            pe.wait_ge(route, ROUTE_BOTH)
            chosen = both.rearrange("p t e -> p (t e)")
            pe.matmul(pv[:, 0:P], tri, chosen, start=True, stop=True)
            pe.matmul(pv[:, P:2 * P], ones_m, chosen, start=True, stop=True).then_inc(count_mm, 1)

            def expert(t):
                return nc.values_load(expert_of[0:1, bass.ds(t, 1)], engines=[mybir.EngineType.PE], min_val=0, max_val=E - 1,
                                      skip_runtime_bounds_check_because="the table is clamped to the experts")

            def turn_rows(n):
                pe.wait_ge(xt_in, n * 16)
                for k in range(KD):
                    last = pe.transpose(pm[:, k * P:(k + 1) * P], xt[:, k * P:(k + 1) * P], ident[:, :])
                last.then_inc(xt_mm, 1)

            def up(t, e):
                pe.wait_ge(xt_ready, t + 1)
                for n in range(2):
                    for k in range(KD):
                        last = pe.matmul(pa[:, n, :], xtT[:, k, :],
                                         w1_v[:, bass.ds(e, 1), k, n * 512:(n + 1) * 512].rearrange("p a f -> p (a f)"),
                                         start=(k == 0), stop=(k == KD - 1))
                    last.then_inc(h_mm, 1)

            def down(n, e):
                pe.wait_ge(hgT_ready, n * 2)
                for k in range(KF):
                    last = pe.matmul(pv[:, 0:D], hgT[:, k, :], w2_v[:, bass.ds(e, 1), k, :].rearrange("p a d -> p (a d)"),
                                     start=(k == 0), stop=(k == KF - 1))
                last.then_inc(y_mm, 1)

            def turn_hidden(t):
                for n in range(2):
                    pe.wait_ge(hg_ready, t * 2 + n + 1)
                    for k in range(KF // 2):
                        q = n * (KF // 2) + k
                        last = pe.transpose(pb[:, n, k * P:(k + 1) * P], hg[:, q * P:(q + 1) * P], ident[:, :])
                    last.then_inc(hgT_mm, 1)

            pe.wait_ge(table_ready, 1)
            turn_rows(1)
            pe.wait_ge(experts_in, 2 * E * 16)
            up(0, expert(0))
            turn_rows(2)
            turn_hidden(0)
            with pe.Fori(1, SLOT_TILES) as t:
                e_before = expert(t - 1)
                e = expert(t)
                up(t, e)
                turn_rows(t + 2)
                down(t, e_before)
                turn_hidden(t)
            down(SLOT_TILES, expert(SLOT_TILES - 1))


MADE = 9
ROUTE_BOTH = 12
ROUTE_DIFF = 13
ROUTE_STEPS = ROUTE_DIFF + 14 + 2 * TOPK + 2 + 3


def kernel(**inputs):
    import numpy as np
    import concourse.bacc as bacc
    from concourse.bass_utils import run_bass_kernel_spmd

    def a(name, pre="L0_"):
        return np.asarray(inputs[pre + name])

    def turned(w, *axes):
        return np.ascontiguousarray(w.transpose(*axes)) if axes else np.ascontiguousarray(w.T)

    mask = a("mask_1x1xSxS2_bk1", "").reshape(S, SC)
    arrays = {
        "x": np.ascontiguousarray(a("x", "").reshape(T, D)),
        "ctxT": turned(a("ctx_1024", "").reshape(B * SC, D)),
        "maskT": turned(mask),
        "wk": turned(a("attn_Wk")), "bk": a("attn_bk"), "wka": turned(a("attn_Wka")), "bka": a("attn_bka"),
        "wv": turned(a("attn_Wv")), "bv": a("attn_bv"), "gamma": a("attn_gamma"), "beta": a("attn_beta"),
        "wq": turned(a("xattn_W_q")), "wxk": turned(a("xattn_W_k")), "wxv": turned(a("xattn_W_v")), "wo": turned(a("xattn_W_o")),
        "rw": turned(a("ffn_router_w")), "rb": a("ffn_router_b"),
        "w1": turned(a("ffn_w1"), 0, 2, 1), "b1": a("ffn_b1"), "w2": turned(a("ffn_w2"), 0, 2, 1), "b2": a("ffn_b2"),
        "lnw": a("ffn_ln_w"), "lnb": a("ffn_ln_b"),
    }
    nc = bacc.Bacc("TRN2", target_bir_lowering=False, num_devices=1)
    args = {n: nc.dram_tensor(f"in_{n}", v.shape, mybir.dt.from_np(v.dtype), kind="ExternalInput").ap()
            for n, v in arrays.items()}
    result = nc.dram_tensor("out", (T, D), F32, kind="ExternalOutput").ap()
    decoder_layer(nc, out=result, **args)
    r = run_bass_kernel_spmd(nc, [{f"in_{n}": v for n, v in arrays.items()}], core_ids=[0])
    return np.asarray(r.results[0]["out"]).reshape(B, S, D)
```

```python
from contextlib import ExitStack

import concourse.bass as bass
from concourse import mybir

F32 = mybir.dt.float32
BF16 = mybir.dt.bfloat16
F16 = mybir.dt.float16
I32 = mybir.dt.int32
U32 = mybir.dt.uint32
U8 = mybir.dt.uint8
ALU = mybir.AluOpType
ACT = mybir.ActivationFunctionType
AX = mybir.AxisListType

P = 128
B, S, D = 2, 1024, 256
T = B * S
KD = D // P
TILES = T // P
CT = 4
CHUNK = CT * P
CPB = S // CHUNK
CHUNKS = T // CHUNK
SC = 77
HEADS, DK = 16, 16
HC = P // DK
HG = 4
VW = DK + 1
E, FF = 8, 1024
KF = FF // P
TOPK = 2
SLOT_TILES = TOPK * T // P + E - 1
XS_TILES = SLOT_TILES + 1
LOW = 2 ** 11
PAIRS = TOPK * TILES
EPS = 1e-5
EPS_FFN = 1e-12
MASKED = -1e30
QUADS = HEADS // 4
STEPS = CT * QUADS
RING = 4
CARRIES = 2 * CHUNKS + 1
GROUPS = TILES // CT


def decoder_layer(nc, x, ctxT, maskT, wk, bk, wka, bka, wv, bv, gamma, beta, wq, wxk, wxv, wo,
                  rw, rb, w1, b1, w2, b2, lnw, lnb, out):
    x2_dram = nc.dram_tensor("x2_rows", [T, D], F32).ap()
    sums = nc.dram_tensor("sums", [T + P, D], F32).ap()

    def tiles(rows):
        return rows.rearrange("(t p) d -> p t d", p=P)

    x_rows, out_rows, x2_rows, sum_rows = tiles(x), tiles(out), tiles(x2_dram), tiles(sums[0:T, :])

    with ExitStack() as ctx:
        def sb(name, shape, dt=F32):
            return ctx.enter_context(nc.sbuf_tensor(name, shape, dt))

        def sem(name):
            return ctx.enter_context(nc.semaphore(name))

        W1 = sb("expert_w1", [P, E * KD * FF])
        W2 = sb("expert_w2", [P, E * KF * D])
        LATE = sb("front_weights_then_b1", [P, E * FF])
        X2 = sb("x2", [P, TILES, D])
        R = sb("work", [P, 5888])
        w1_v = W1[:, :].rearrange("p (e k f) -> p e k f", e=E, k=KD)
        w2_v = W2[:, :].rearrange("p (e k n) -> p e k n", e=E, k=KF)
        EW = KD * FF
        EARLY = 5

        def slot(n):
            t, m = (W1, n) if n < 6 else (W2, n - 6)
            return t[:, EARLY * EW + m * 1024:EARLY * EW + (m + 1) * 1024]

        def by_tile(ap):
            return ap.rearrange("p (j d) -> p j d", j=CT)

        def by_chunk(ap):
            return ap.rearrange("p (k n) -> p k n", k=KD)

        xc = by_tile(slot(0))
        h0 = by_tile(slot(1))
        hT = by_chunk(slot(2))
        x1T = by_chunk(slot(2))
        keysT = by_chunk(slot(3))
        kexp = by_chunk(slot(4))
        csum = by_chunk(slot(5))
        kw = by_chunk(slot(6))
        attnT = by_chunk(slot(6))
        pooled = by_chunk(slot(7))
        r2 = by_tile(slot(8))
        x1 = by_tile(slot(9))
        x2c = by_tile(slot(10))
        qT = by_chunk(slot(11))

        off = [0]

        def late(n):
            off[0] += n
            return LATE[:, off[0] - n:off[0]]

        def late_w():
            return late(KD * D).rearrange("p (k n) -> p k n", k=KD)

        wk_s, wka_s, wv_s, wq_s, wxk_s, wxv_s, wo_s = (late_w() for _ in range(7))
        B1_EARLY = 6 * KD * D // FF
        kbd = late(B * HEADS * SC).rearrange("p (b c h k) -> p b c h k", b=B, c=KD, h=HC)
        vaug = late(B * HEADS * VW).rearrange("p (b h v) -> p b h v", b=B, h=HEADS)
        ctx_s = late(KD * B * SC).rearrange("p (k n) -> p k n", k=KD)
        rw_s = late(KD * E).rearrange("p (k e) -> p k e", k=KD)
        rb_s = late(E)
        assert off[0] <= E * FF
        b1_s = LATE[:, :].rearrange("p (e f) -> p e f", e=E)

        prob = R[:, 0:1232].rearrange("p (s h k) -> p s h k", s=RING, h=HG)
        probT = R[:, 1232:3280].rearrange("p (s h q) -> p s h q", s=RING, h=HG)
        merged = R[:, 3280:3792].rearrange("p (s d) -> p s d", s=2)
        mergedT = R[:, 3792:4304].rearrange("p (s k q) -> p s k q", s=2, k=KD)
        x2T = by_chunk(R[:, 4304:5328])
        xt = R[:, 0:256]
        xtT = R[:, 256:512].rearrange("p (k q) -> p k q", k=KD)
        hb = R[:, 512:1536]
        hg = R[:, 1536:2560]
        hgT = R[:, 2560:3584].rearrange("p (k q) -> p k q", k=KF)
        yt = R[:, 3584:3840]
        b2_s = R[:, 3840:5888].rearrange("p (e d) -> p e d", e=E)
        total = W1[:, 0:TILES * D].rearrange("p (t d) -> p t d", t=TILES)
        zed = W2[:, 6656:7680].rearrange("p (j d) -> p j d", j=CT)
        fin = W2[:, 2048:6144].rearrange("p (t d) -> p t d", t=TILES)
        lnw_s = W2[:, 6144:6144 + D]
        lnb_s = W2[:, 6400:6400 + D]

        ident = sb("identity", [P, P])
        mask_b = sb("mask_bias", [P, S], BF16)
        mask_raw = slot(11)[0:SC, 0:S // 4].bitcast(U8)
        eye4 = sb("identity_per_head", [P, HG, SC], BF16)
        gam = sb("gamma", [P, KD])
        bet = sb("beta", [P, KD])
        bk_s = sb("bk", [P, KD])
        bka_s = sb("bka", [P, KD])
        bv_s = sb("bv", [P, KD])
        norms = []
        for n in range(3):
            norm = {m: sb(f"ln{n}_{m}", [P, CT]) for m in ("mdiff", "msum", "vsum", "msq", "mean", "veps", "rstd")}
            norm["stats"] = sb(f"ln{n}_stats", [P, CT, 6])
            norm.update((m, sem(f"ln{n}_{m}")) for m in ("stats_done", "moments_done", "var_ready", "rstd_ready"))
            norms.append(norm)
        LN1, LN2, LN3 = norms
        OUT_NORMS = LN1, LN3
        neg_mean, shift = sb("neg_mean", [P, CT]), sb("norm_shift", [P, CT])
        carry = sb("carry", [P, CARRIES, 2, KD])
        start = sb("chunk_start", [P, 2, KD])
        mhalf = sb("minus_half", [P, CT])
        one_c = sb("one", [P, 1])
        smax = sb("score_max", [P, 2, HEADS])
        psum_r = sb("prob_sum_recip", [P, HEADS])
        pscale = sb("prob_scale", [P, HEADS])
        logits = sb("logits", [P, TILES, E])
        weight = sb("choice_weight", [P, TOPK, TILES])
        token_of = sb("token_of_slot", [P, XS_TILES], U32)
        sum_of = sb("sum_of_slot", [P, XS_TILES], U32)
        weight_of = sb("weight_of_slot", [P, XS_TILES])
        load_rows = sb("load_rows", [P, 1], U32)
        add_rows = sb("add_rows", [P, 1], U32)
        expert_of = sb("expert_of_tile", [P, XS_TILES], I32)

        at = [0]

        def tmp(*shape):
            n = 1
            for m in shape:
                n *= m
            at[0] += n
            assert at[0] <= 5888
            v = R[:, at[0] - n:at[0]]
            if len(shape) == 2:
                v = v.rearrange("p (a b) -> p a b", a=shape[0])
            return v

        m1, m2, first = tmp(TILES), tmp(TILES), tmp(TILES)
        hot = [tmp(TILES, E) for _ in range(TOPK)]
        cand, rest = tmp(TILES, E), tmp(TILES, E)
        both = tmp(TILES, E)
        ex, den = tmp(TILES), tmp(TILES)
        tot, run = tmp(E, TILES), tmp(E, TILES)
        ones_r = tmp(E * TILES)
        starts, count, ntile, tbend, adj = tmp(E), tmp(E), tmp(E), tmp(E), tmp(E)
        counti = tmp(E)
        slots = tmp(TILES, E)
        picked = tmp(TILES, E)
        slotf = tmp(TOPK, TILES)
        sloti, tilei, posi = tmp(PAIRS), tmp(PAIRS), tmp(PAIRS)
        tile_n, pos_n = tmp(PAIRS), tmp(PAIRS)
        token1 = tmp(TILES + 1)
        cols = tmp(P)
        at_pos = tmp(4 * P // 2).bitcast(F16).rearrange("p (s m) -> p s m", s=4)
        assert T <= 2048
        marks = tmp(3 * PAIRS * XS_TILES // 2).bitcast(F16).rearrange("p (m i t) -> p m i t", m=3, i=PAIRS)
        at_tile = tmp(PAIRS * XS_TILES // 2).bitcast(F16).rearrange("p (i t) -> p i t", i=PAIRS)
        token1h = tmp(TILES // 2).bitcast(F16)
        w_hi, w_lo = tmp(PAIRS // 2).bitcast(F16), tmp(PAIRS // 2).bitcast(F16)
        w_rest = tmp(PAIRS)
        empty, loadf = tmp(XS_TILES), tmp(XS_TILES)
        rev = tmp(E)
        tau = tmp(XS_TILES, E)
        tge = tmp(XS_TILES, E)
        tri = tmp(P)
        ones_m = tmp(P)
        tilef = tmp(XS_TILES)

        hmask = slot(8)[:, 0:HC]

        pa = ctx.enter_context(nc.psum_tensor("psum_a", [P, KD, 512], F32))
        pb = ctx.enter_context(nc.psum_tensor("psum_b", [P, KD, 512], F32))
        pc = ctx.enter_context(nc.psum_tensor("psum_c", [P, KD, 512], F32))
        pv = ctx.enter_context(nc.psum_tensor("psum_v", [P, 512], F32))
        pm = ctx.enter_context(nc.psum_tensor("psum_m", [P, 512], F32))
        pb_t = pb[:, :, :].rearrange("p a (b d) -> p (a b) d", d=D)

        (consts_in, weights_in, ctx_in, experts_in, late_in, b2_in, ln_in, made, mask_made,
         ctx_mm, kv_made, x_in, x_free, h0_ready, hT_mm, hT_ready, k_mm, kT_ready, ka_mm, kexp_ready, started, key_sum,
         kk_ready, recip_ready, kw_ready, pooled_ready, v_mm, attn_ready, at_mm, x1_ready, x1_kept, x1T_mm, x1T_ready,
         q_mm, qT_ready, s_mm, max_ready, sub_ready, exp_ready, pT_mm, pT_ready, pv_mm, rec_ready, scale_ready,
         merged_ready, mT_mm, mT_ready, o_mm, r2_ready, x2_ready, x2_kept, x2T_mm, x2T_ready, lg_mm, lg_ready,
         bka_ready, carry_zero) = (sem(n) for n in (
             "consts_in weights_in ctx_in experts_in late_in b2_in ln_in made mask_made "
             "ctx_mm kv_made x_in x_free h0_ready hT_mm hT_ready k_mm kT_ready ka_mm kexp_ready started key_sum "
             "kk_ready recip_ready kw_ready pooled_ready v_mm attn_ready at_mm x1_ready x1_kept x1T_mm x1T_ready "
             "q_mm qT_ready s_mm max_ready sub_ready exp_ready pT_mm pT_ready pv_mm rec_ready scale_ready "
             "merged_ready mT_mm mT_ready o_mm r2_ready x2_ready x2_kept x2T_mm x2T_ready lg_mm lg_ready "
             "bka_ready carry_zero").split())
        (route_consts, route, ex_ready, count_mm, pos_ready, pos_mm, x2_out, load_set, add_set, table_ready, base_ready, yb_ready, neg_mean_ready, shift_ready, xt_in, xt_mm, xt_ready, h_mm,
         hb_ready, hg_ready, hgT_mm, hgT_ready, y_mm, y_ready, y_out, fin_step, fin_ready, fin_out) = (
            sem(n) for n in (
                "route_consts route ex_ready count_mm pos_ready pos_mm x2_out load_set add_set table_ready base_ready yb_ready neg_mean_ready shift_ready xt_in xt_mm xt_ready h_mm "
                "hb_ready hg_ready hgT_mm hgT_ready y_mm y_ready y_out fin_step fin_ready fin_out").split())
        sum_in = [sem(f"sum_in{g}") for g in range(GROUPS)]

        block = ctx.enter_context(nc.Block())

        @block.sync
        def _(sp):
            sp.dma_start(xc, x_rows[:, 0:CT, :]).then_inc(x_in, 16)
            for dst, src in ((gam, gamma), (bet, beta), (bk_s, bk), (bka_s, bka), (bv_s, bv)):
                with nc.allow_non_contiguous_dma(reason="256 values, one per partition"):
                    sp.dma_start(dst[:, :], src.rearrange("(k p) -> p k", p=P)).then_inc(consts_in, 16)
            for dst, src in ((wk_s, wk), (wka_s, wka), (wv_s, wv)):
                sp.dma_start(dst, src.rearrange("(k p) n -> p k n", p=P)).then_inc(weights_in, 16)
            sp.dma_start(ctx_s, ctxT.rearrange("(k p) n -> p k n", p=P)).then_inc(ctx_in, 16)
            sp.dma_start(mask_raw, maskT).then_inc(ctx_in, 16)
            for dst, src in ((wxk_s, wxk), (wxv_s, wxv), (wq_s, wq), (wo_s, wo)):
                sp.dma_start(dst, src.rearrange("(k p) n -> p k n", p=P)).then_inc(ctx_in, 16)
            sp.dma_start(rw_s, rw.rearrange("(k p) e -> p k e", p=P)).then_inc(ctx_in, 16)
            sp.dma_start(rb_s, rb.partition_broadcast(P)).then_inc(ctx_in, 16)
            for e in range(EARLY):
                sp.dma_start(w1_v[:, e], w1[e].rearrange("(k p) f -> p k f", p=P)).then_inc(experts_in, 16)
                sp.dma_start(w2_v[:, e], w2[e].rearrange("(k p) d -> p k d", p=P)).then_inc(experts_in, 16)

            def load_chunk(n):
                sp.wait_ge(x_free, n)
                sp.dma_start(xc, x_rows[:, bass.ds(n * CT, CT), :]).then_inc(x_in, 16)

            def store_x2(it):
                sp.wait_ge(x2_kept, it + 1)
                for rows in (x2_rows, sum_rows):
                    sp.dma_start(rows[:, bass.ds(it * CT, CT), :], X2[:, bass.ds(it * CT, CT), :]).then_inc(x2_out, 16)

            load_chunk(1)
            with sp.Fori(1, CHUNKS - 1) as it:
                load_chunk(it + 1)
                store_x2(it - 1)
            sp.wait_ge(qT_ready, CHUNKS)
            for e in range(EARLY, E):
                sp.dma_start(w1_v[:, e], w1[e].rearrange("(k p) f -> p k f", p=P)).then_inc(experts_in, 16)
            sp.dma_start(b1_s[:, 0:B1_EARLY], b1[0:B1_EARLY].partition_broadcast(P)).then_inc(late_in, 16)
            store_x2(CHUNKS - 2)
            sp.dma_start(tiles(sums)[:, TILES, :], X2[:, 0, :]).then_inc(x2_out, 16)
            sp.wait_ge(lg_ready, CHUNKS)
            store_x2(CHUNKS - 1)
            for e in range(EARLY, E):
                sp.dma_start(w2_v[:, e], w2[e].rearrange("(k p) d -> p k d", p=P)).then_inc(experts_in, 16)
            sp.dma_start(b1_s[:, B1_EARLY:E], b1[B1_EARLY:E].partition_broadcast(P)).then_inc(late_in, 16)
            sp.wait_ge(xt_mm, 1)
            sp.dma_start(R[:, 3840:5888], b2.rearrange("e d -> (e d)").partition_broadcast(P)).then_inc(b2_in, 16)

            sp.wait_ge(y_ready, SLOT_TILES)
            sp.dma_start(lnw_s, lnw.partition_broadcast(P)).then_inc(ln_in, 16)
            sp.dma_start(lnb_s, lnb.partition_broadcast(P)).then_inc(ln_in, 16)
            sp.wait_ge(y_out, 16 * SLOT_TILES)
            for g in range(GROUPS):
                sp.dma_start(total[:, g * CT:(g + 1) * CT, :], sum_rows[:, g * CT:(g + 1) * CT, :]).then_inc(sum_in[g], 16)
            for g in range(GROUPS):
                sp.wait_ge(fin_ready, g + 1)
                sp.dma_start(out_rows[:, g * CT:(g + 1) * CT, :], fin[:, g * CT:(g + 1) * CT, :]).then_inc(fin_out, 16)
            sp.wait_ge(fin_out, 16 * GROUPS)
            sp.wait_ge(xt_in, 16 * XS_TILES)

        @block.gpsimd
        def _(pool):
            pool.memset(mhalf[:, :], -0.5).then_inc(made, 1)
            pool.memset(ident[:, :], 0.0).then_inc(made, 1)
            pool.memset(eye4[:, :, :], 0.0).then_inc(made, 1)
            pool.memset(hmask, 1.0).then_inc(made, 1)
            pool.memset(one_c[:, :], 1.0).then_inc(made, 1)
            pool.wait_ge(made, 5)
            pool.affine_select(out=ident[:, :], in_=ident[:, :], compare_op=ALU.not_equal, fill=1.0, base=0,
                               pattern=[[-1, P]], channel_multiplier=1).then_inc(made, 1)
            pool.affine_select(out=eye4[:, :, :], in_=eye4[:, :, :], compare_op=ALU.not_equal, fill=1.0, base=0,
                               pattern=[[0, HG], [-1, SC]], channel_multiplier=1).then_inc(made, 1)
            pool.affine_select(out=hmask, in_=hmask, compare_op=ALU.is_ge, fill=0.0, base=0,
                               pattern=[[-DK, HC]], channel_multiplier=1).then_inc(made, 1)
            pool.wait_ge(made, 8)
            pool.affine_select(out=hmask, in_=hmask, compare_op=ALU.is_ge, fill=0.0, base=DK - 1,
                               pattern=[[DK, HC]], channel_multiplier=-1).then_inc(made, 1)

            def rsqrt(norm, count):
                pool.wait_ge(norm["var_ready"], count)
                pool.tensor_tensor(norm["rstd"][:, :], norm["veps"][:, :], mhalf[:, :], ALU.pow).then_inc(norm["rstd_ready"], 1)

            def output(it):
                rsqrt(LN3, it + 1)
                pool.wait_ge(x2_ready, it + 1)
                pool.tensor_copy(X2[:, bass.ds(it * CT, CT), :], x2c).then_inc(x2_kept, 1)

            def self_attention(n, prev=None):
                rsqrt(LN1, n + 1)
                if prev is not None:
                    output(prev)
                pool.wait_ge(key_sum, n + 1)
                pool.tensor_tensor(kexp, kexp, keysT, ALU.mult).then_inc(kk_ready, 1)
                rsqrt(LN2, n + 1)
                pool.wait_ge(x1_ready, n + 1)
                pool.tensor_copy(X2[:, bass.ds(n * CT, CT), :], x1).then_inc(x1_kept, 1)

            self_attention(0)
            self_attention(1)
            with pool.Fori(1, CHUNKS - 1) as it:
                self_attention(it + 1, it - 1)
            output(CHUNKS - 2)
            output(CHUNKS - 1)

            pool.wait_ge(lg_ready, CHUNKS)
            pool.iota(tau, pattern=[[1, XS_TILES], [0, E]], base=0, channel_multiplier=0,
                      allow_small_or_imprecise_dtypes=True).then_inc(route_consts, 1)
            pool.iota(rev, pattern=[[-1, E]], base=E, channel_multiplier=0,
                      allow_small_or_imprecise_dtypes=True).then_inc(route_consts, 1)
            pool.memset(ones_m, 1.0).then_inc(route_consts, 1)
            pool.memset(ones_r, 1.0).then_inc(route_consts, 1)
            pool.iota(cols, pattern=[[1, P]], base=0, channel_multiplier=0,
                      allow_small_or_imprecise_dtypes=True).then_inc(route_consts, 1)
            pool.iota(token1, pattern=[[P, TILES + 1]], base=1, channel_multiplier=1,
                      allow_small_or_imprecise_dtypes=True).then_inc(route_consts, 1)
            pool.wait_ge(route_consts, 6)
            pool.affine_select(out=tri, in_=ones_m, compare_op=ALU.is_gt, fill=0.0, base=0,
                               pattern=[[1, P]], channel_multiplier=-1).then_inc(route_consts, 1)

            def load_tile(idx):
                pool.indirect_dma_start(xt, None, x2_dram, bass.IndirectOffsetOnAxis(idx, 0)).then_inc(xt_in, 16)

            def add_tile(idx):
                pool.indirect_dma_start(sums, bass.IndirectOffsetOnAxis(idx, 0), yt, None,
                                        compute_op=ALU.add).then_inc(y_out, 16)

            pool.wait_ge(table_ready, TABLES)
            pool.wait_ge(x2_out, (2 * CHUNKS + 1) * 16)
            load_tile(token_of[:, 0:1])
            pool.wait_ge(xt_mm, 1)
            load_tile(token_of[:, 1:2])
            with pool.Fori(1, SLOT_TILES) as t:
                pool.wait_ge(xt_mm, t + 1)
                pool.tensor_copy(load_rows[:, :], token_of[:, bass.ds(t + 1, 1)]).then_inc(load_set, 1)
                pool.wait_ge(x2_out, (2 * CHUNKS + 1) * 16)
                pool.wait_ge(load_set, t)
                load_tile(load_rows[:, :])
                pool.wait_ge(y_ready, t)
                pool.tensor_copy(add_rows[:, :], sum_of[:, bass.ds(t - 1, 1)]).then_inc(add_set, 1)
                pool.wait_ge(x2_out, (2 * CHUNKS + 1) * 16)
                pool.wait_ge(add_set, t)
                add_tile(add_rows[:, :])
            pool.wait_ge(y_ready, SLOT_TILES)
            add_tile(sum_of[:, SLOT_TILES - 1:SLOT_TILES])
            pool.wait_ge(xt_in, 16 * XS_TILES)

            def base(g):
                pool.tensor_tensor(fin[:, g * CT:(g + 1) * CT, :], X2[:, g * CT:(g + 1) * CT, :],
                                   lnb_s.rearrange("p (j d) -> p j d", j=1).to_broadcast([P, CT, D]),
                                   ALU.add).then_inc(base_ready, 1)

            def last_scale(g):
                rsqrt(LN2, CHUNKS + g + 1)
                pool.wait_ge(LN2["rstd_ready"], CHUNKS + g + 1)
                pool.wait_ge(neg_mean_ready, g + 1)
                pool.tensor_tensor(shift[:, :], neg_mean[:, :], LN2["rstd"][:, :], ALU.mult).then_inc(shift_ready, 1)

            pool.wait_ge(ln_in, 2 * 16)
            for g in range(GROUPS):
                base(g)
                rsqrt(OUT_NORMS[g % 2], CHUNKS + g // 2 + 1)
                if g >= 1:
                    last_scale(g - 1)
            last_scale(GROUPS - 1)

        @block.scalar
        def _(act):
            act.wait_ge(consts_in, 5 * 16)
            act.mul(bka_s[:, :], bka_s[:, :], D ** -0.5).then_inc(bka_ready, 1)
            act.wait_ge(bka_ready, 1)

            def normalised(n):
                act.wait_ge(hT_mm, n + 1)
                for k in range(KD):
                    last = act.activation(hT[:, k, :], pb[:, k, :], ACT.Identity, scale=gam[:, k:k + 1],
                                          bias=bet[:, k:k + 1])
                last.then_inc(hT_ready, 1)

            def keys(n):
                act.wait_ge(k_mm, n + 1)
                for k in range(KD):
                    last = act.activation(keysT[:, k, :], pb[:, k, :], ACT.Identity, bias=bk_s[:, k:k + 1])
                last.then_inc(kT_ready, 1)

            def key_weights(n):
                act.wait_ge(ka_mm, n + 1)
                for k in range(KD):
                    last = act.activation(kexp[:, k, :], pb[:, k, :], ACT.Exp, scale=D ** -0.5, bias=bka_s[:, k:k + 1])
                last.then_inc(kexp_ready, 1)

            def x1_features(n):
                act.wait_ge(x1T_mm, n + 1)
                act.activation(x1T, pb[:, :, :], ACT.Copy).then_inc(x1T_ready, 1)

            def queries(n):
                act.wait_ge(q_mm, n + 1)
                act.activation(qT, pb[:, :, :], ACT.Copy).then_inc(qT_ready, 1)

            def output_features(it):
                act.wait_ge(x2T_mm, it + 1)
                act.activation(x2T, pb[:, :, :], ACT.Copy).then_inc(x2T_ready, 1)

            def cross_attention(it, nxt, prev):
                def turned_probs(h):
                    act.wait_ge(pT_mm, it * STEPS + h + 1)
                    act.activation(probT[0:SC, h % RING], pc[0:SC, h % 2, :].rearrange("p (h q) -> p h q", h=HG),
                                   ACT.Copy).then_inc(pT_ready, 1)

                def turned_heads(j):
                    act.wait_ge(mT_mm, it * CT + j + 1)
                    act.activation(mergedT[:, j % 2], pm[:, 0:D].rearrange("p (k q) -> p k q", k=KD),
                                   ACT.Copy).then_inc(mT_ready, 1)

                for h in range(STEPS):
                    act.wait_ge(sub_ready, it * STEPS + h + 1)
                    act.activation(prob[:, h % RING], prob[:, h % RING], ACT.Exp, scale=DK ** -0.5).then_inc(exp_ready, 1)
                    if h >= 1:
                        turned_probs(h - 1)
                    if h >= QUADS and h % QUADS == 2:
                        turned_heads(h // QUADS - 1)
                    if nxt is not None:
                        if h == 3:
                            normalised(nxt)
                        if h == 4:
                            keys(nxt)
                        if h == 5:
                            key_weights(nxt)
                        if h == 15:
                            x1_features(nxt)
                    if prev is not None and h == 7:
                        output_features(prev)
                turned_probs(STEPS - 1)
                turned_heads(CT - 1)
                if nxt is not None:
                    queries(nxt)

            for stage in (normalised, keys, key_weights, x1_features, queries):
                stage(0)
            cross_attention(0, 1, None)
            with act.Fori(1, CHUNKS - 1) as it:
                cross_attention(it, it + 1, it - 1)
            cross_attention(CHUNKS - 1, None, CHUNKS - 2)
            output_features(CHUNKS - 1)

            act.wait_ge(route, ROUTE_DIFF)
            act.activation(ex, ex, ACT.Exp).then_inc(ex_ready, 1)

            def turned_rows(n):
                act.wait_ge(xt_mm, n)
                act.activation(xtT, pm[:, 0:D].rearrange("p (k q) -> p k q", k=KD), ACT.Copy).then_inc(xt_ready, 1)

            act.preload_act_table(ACT.Gelu)
            turned_rows(1)
            with act.Fori(0, SLOT_TILES) as t:
                for n in range(2):
                    act.wait_ge(hb_ready, t * 2 + n + 1)
                    act.activation(hg[:, n * 512:(n + 1) * 512], hb[:, n * 512:(n + 1) * 512],
                                   ACT.Gelu).then_inc(hg_ready, 1)
                turned_rows(t + 2)
                act.wait_ge(hgT_mm, t * 2 + 1)
                act.activation(hgT[:, 0:KF // 2, :], pb[:, 0, :].rearrange("p (k q) -> p k q", k=KF // 2),
                               ACT.Copy).then_inc(hgT_ready, 1)

            for g in range(GROUPS):
                act.wait_ge(shift_ready, g + 1)
                for j in range(CT):
                    last = act.activation(fin[:, g * CT + j, :], fin[:, g * CT + j, :], ACT.Identity,
                                          scale=LN2["rstd"][:, j:j + 1], bias=shift[:, j:j + 1])
                last.then_inc(fin_ready, 1)

        @block.vector
        def _(dve):
            def moments(norm, src, eps, count):
                stats = norm["stats"]
                for j in range(CT):
                    last = dve.bn_stats(stats[:, j, :], src[:, j, :])
                last.then_inc(norm["stats_done"], 1)
                mean_e, mean_o, var_e, var_o = stats[:, :, 1], stats[:, :, 4], stats[:, :, 2], stats[:, :, 5]
                dve.wait_ge(norm["stats_done"], count)
                dve.tensor_tensor(norm["mdiff"][:, :], mean_e, mean_o, ALU.subtract)
                dve.tensor_tensor(norm["msum"][:, :], mean_e, mean_o, ALU.add)
                dve.scalar_tensor_tensor(norm["vsum"][:, :], var_e, D * eps, var_o, ALU.add,
                                         ALU.add).then_inc(norm["moments_done"], 1)
                dve.wait_ge(norm["moments_done"], 2 * count - 1)
                dve.scalar_tensor_tensor(norm["msq"][:, :], norm["mdiff"][:, :], 0.25, norm["mdiff"][:, :], ALU.mult, ALU.mult)
                dve.tensor_scalar(norm["mean"][:, :], norm["msum"][:, :], 0.5, None, ALU.mult).then_inc(norm["moments_done"], 1)
                dve.wait_ge(norm["moments_done"], 2 * count)
                dve.scalar_tensor_tensor(norm["veps"][:, :], norm["vsum"][:, :], 1.0 / D, norm["msq"][:, :], ALU.mult,
                                         ALU.add).then_inc(norm["var_ready"], 1)

            def normalise(norm, src, dst, count, done):
                dve.wait_ge(norm["rstd_ready"], count)
                for j in range(CT):
                    last = dve.tensor_scalar(dst[:, j, :], src[:, j, :], norm["mean"][:, j:j + 1], norm["rstd"][:, j:j + 1],
                                             ALU.subtract, ALU.mult)
                last.then_inc(done, 1)

            def context():
                dve.wait_ge(ctx_in, 8 * 16)
                dve.tensor_scalar(mask_b[0:SC, :], mask_raw, MASKED, None, ALU.mult).then_inc(mask_made, 1)
                dve.memset(vaug[0:SC], 1.0).then_inc(mask_made, 1)
                dve.wait_ge(made, MADE)
                dve.wait_ge(mask_made, 2)
                dve.wait_ge(ctx_mm, 1)
                for c in range(KD):
                    for b in range(B):
                        keys = pa[:, c, b * SC:(b + 1) * SC].rearrange("p (h k) -> p h k", h=1).to_broadcast([P, HC, SC])
                        dve.tensor_tensor(kbd[:, b, c], keys, hmask.rearrange("p (h k) -> p h k", k=1).to_broadcast([P, HC, SC]),
                                          ALU.mult)
                for b in range(B):
                    last = dve.tensor_copy(vaug[0:SC, b, :, 0:DK], pc[0:SC, b, 0:D].rearrange("p (h v) -> p h v", h=HEADS))
                last.then_inc(kv_made, 1)

            dve.wait_ge(made, MADE)
            one_s = one_c[:, 0:1].to_broadcast([P, CHUNK])
            dve.memset(carry[:, :, :, :], 0.0).then_inc(carry_zero, 1)
            dve.wait_ge(carry_zero, 1)

            def kept_in(n):
                return bass.ds(n + 1 + (n % CPB) * CHUNKS, 1)

            def input_moments(n):
                dve.wait_ge(x_in, n * 16 + 16)
                moments(LN1, xc, EPS, n + 1)

            def input_normalise(n):
                normalise(LN1, xc, h0, n + 1, h0_ready)

            def sum_weights(n):
                dve.tensor_copy(start[:, :, :], carry[:, bass.ds(n, 1)].rearrange("p a s k -> p (a s) k")).then_inc(started, 1)
                dve.wait_ge(kexp_ready, n + 1)
                dve.wait_ge(started, n + 1)
                for k in range(KD):
                    last = dve.tensor_tensor_scan(csum[:, k, :], one_s, kexp[:, k, :], start[:, 0, k:k + 1], ALU.mult, ALU.add)
                last.then_inc(key_sum, 1)
                dve.wait_ge(key_sum, n + 1)

            def invert(n, part):
                cols = slice(part % 2 * CHUNK // 2, (part % 2 + 1) * CHUNK // 2)
                dve.reciprocal(kw[:, part // 2, cols], csum[:, part // 2, cols]).then_inc(recip_ready, 1)

            def weigh_keys(n):
                dve.wait_ge(recip_ready, n * 4 + 4)
                dve.wait_ge(kk_ready, n + 1)
                dve.tensor_tensor(kw, kw, kexp, ALU.mult).then_inc(kw_ready, 1)

            def pool_keys(n):
                dve.wait_ge(kw_ready, n + 1)
                for k in range(KD):
                    last = dve.tensor_tensor_scan(pooled[:, k, :], one_s, kw[:, k, :], start[:, 1, k:k + 1], ALU.mult, ALU.add)
                last.then_inc(pooled_ready, 1)
                dve.wait_ge(pooled_ready, n + 1)
                dve.tensor_copy(carry[:, kept_in(n), 0].rearrange("p a k -> p (a k)"), csum[:, :, CHUNK - 1])
                dve.tensor_copy(carry[:, kept_in(n), 1].rearrange("p a k -> p (a k)"), pooled[:, :, CHUNK - 1])

            def times_values(n):
                dve.wait_ge(v_mm, n * KD + KD)
                for k in range(KD):
                    last = dve.scalar_tensor_tensor(attnT[:, k, :], pb[:, k, :], bv_s[:, k:k + 1], pooled[:, k, :],
                                                    ALU.add, ALU.mult)
                last.then_inc(attn_ready, 1)

            def x1_moments(n):
                dve.wait_ge(at_mm, n + 1)
                dve.tensor_tensor(h0, pb_t, xc, ALU.add).then_inc(x_free, 1)
                dve.wait_ge(x_free, n + 1)
                moments(LN2, h0, EPS, n + 1)

            def x1_normalise(n):
                normalise(LN2, h0, x1, n + 1, x1_ready)

            def output_moments(it):
                dve.wait_ge(r2_ready, it * CT + CT)
                moments(LN3, r2, EPS, it + 1)

            def output_normalise(it):
                normalise(LN3, r2, x2c, it + 1, x2_ready)

            def route_logits(it):
                dve.wait_ge(lg_mm, it + 1)
                dve.wait_ge(x2_kept, it + 1)
                dve.tensor_tensor(logits[:, bass.ds(it * CT, CT), :], pb[:, 0, 0:CT * E].rearrange("p (j e) -> p j e", j=CT),
                                  rb_s.rearrange("p (j e) -> p j e", j=1).to_broadcast([P, CT, E]),
                                  ALU.add).then_inc(lg_ready, 1)

            def cross_attention(it, nxt, prev):
                def residual(j):
                    dve.wait_ge(x1_kept, it + 1)
                    dve.wait_ge(o_mm, it * CT + j + 1)
                    dve.tensor_tensor(r2[:, j, :], pm[:, D:2 * D], X2[:, bass.ds(it * CT + j, 1), :].rearrange("p a d -> p (a d)"),
                                      ALU.add).then_inc(r2_ready, 1)

                def normalise_heads(j):
                    dve.wait_ge(pv_mm, it * CT + j + 1)
                    sums = pv[:, 0:HEADS * VW].rearrange("p (h v) -> p h v", h=HEADS)
                    dve.reciprocal(psum_r[:, :], sums[:, :, DK]).then_inc(rec_ready, 1)
                    dve.wait_ge(rec_ready, it * CT + j + 1)
                    dve.scalar_tensor_tensor(pscale[:, :], smax[:, j % 2, :], MASKED / 10, psum_r[:, :], ALU.is_gt,
                                             ALU.mult).then_inc(scale_ready, 1)
                    dve.wait_ge(scale_ready, it * CT + j + 1)
                    dve.tensor_tensor(merged[:, j % 2, :].rearrange("p (h v) -> p h v", h=HEADS), sums[:, :, 0:DK],
                                      pscale[:, :].rearrange("p (h v) -> p h v", v=1).to_broadcast([P, HEADS, DK]),
                                      ALU.mult).then_inc(merged_ready, 1)

                for h in range(STEPS):
                    j, quad = divmod(h, QUADS)
                    scores = pa[:, h % 2, 0:HG * SC].rearrange("p (h k) -> p h k", h=HG)
                    top = smax[:, j % 2, quad * HG:(quad + 1) * HG]
                    dve.wait_ge(s_mm, it * STEPS + h + 1)
                    dve.tensor_reduce(top, scores, AX.X, ALU.max).then_inc(max_ready, 1)
                    dve.wait_ge(max_ready, it * STEPS + h + 1)
                    dve.tensor_tensor(prob[:, h % RING], scores,
                                      top.rearrange("p (h k) -> p h k", k=1).to_broadcast([P, HG, SC]),
                                      ALU.subtract).then_inc(sub_ready, 1)
                    if h >= QUADS and quad == 1:
                        normalise_heads(j - 1)
                    if h >= QUADS and quad == QUADS - 1:
                        residual(j - 1)
                    if nxt is not None:
                        if h == 1:
                            input_moments(nxt)
                        if h == 2:
                            input_normalise(nxt)
                        if h == 6:
                            sum_weights(nxt)
                        if h in (7, 8, 9, 10):
                            invert(nxt, h - 7)
                        if h == 10:
                            weigh_keys(nxt)
                        if h == 11:
                            pool_keys(nxt)
                        if h == 12:
                            times_values(nxt)
                        if h == 13:
                            x1_moments(nxt)
                        if h == 14:
                            x1_normalise(nxt)
                    if prev is not None:
                        if h == 3:
                            output_moments(prev)
                        if h == 4:
                            output_normalise(prev)
                        if h == 8:
                            route_logits(prev)
                normalise_heads(CT - 1)
                residual(CT - 1)

            input_moments(0)
            input_normalise(0)
            sum_weights(0)
            for part in range(4):
                invert(0, part)
            weigh_keys(0)
            pool_keys(0)
            times_values(0)
            context()
            x1_moments(0)
            x1_normalise(0)
            cross_attention(0, 1, None)
            with dve.Fori(1, CHUNKS - 1) as it:
                cross_attention(it, it + 1, it - 1)
            cross_attention(CHUNKS - 1, None, CHUNKS - 2)
            output_moments(CHUNKS - 1)
            output_normalise(CHUNKS - 1)
            route_logits(CHUNKS - 1)

            steps = [0]

            def then(ins):
                steps[0] += 1
                ins.then_inc(route, 1)
                dve.wait_ge(route, steps[0])

            def per_e(ap):
                return ap.rearrange("p (a e) -> p a e", a=1).to_broadcast([P, TILES, E])

            def per_t(ap):
                return ap.rearrange("p (t e) -> p t e", e=1).to_broadcast([P, TILES, E])

            dve.wait_ge(lg_ready, CHUNKS)
            dve.wait_ge(route_consts, 7)
            lg = logits[:, :, :]
            for c, (src, top) in enumerate(((lg, m1), (rest, m2))):
                then(dve.tensor_reduce(top, src, AX.X, ALU.max))
                then(dve.tensor_tensor(cand, src, per_t(top), ALU.is_equal))
                then(dve.tensor_tensor(cand, cand, per_e(rev), ALU.mult))
                then(dve.tensor_reduce(first, cand, AX.X, ALU.max))
                then(dve.tensor_tensor(hot[c], cand, per_t(first), ALU.is_equal))
                if c == 0:
                    then(dve.scalar_tensor_tensor(rest, hot[0], -3e38, lg, ALU.mult, ALU.add))
            then(dve.tensor_tensor(both, hot[0], hot[1], ALU.add))
            assert steps[0] == ROUTE_BOTH
            then(dve.tensor_tensor(ex, m2, m1, ALU.subtract))
            assert steps[0] == ROUTE_DIFF
            dve.wait_ge(count_mm, 1)
            then(dve.tensor_copy(tot, pv[:, P:2 * P].rearrange("p (t e) -> p e t", e=E)))
            then(dve.tensor_tensor_scan(run.rearrange("p e t -> p (e t)"), ones_r, tot.rearrange("p e t -> p (e t)"), 0.0,
                                        ALU.mult, ALU.add))
            then(dve.memset(starts[:, 0:1], 0.0))
            then(dve.tensor_copy(starts[:, 1:E], run[:, 0:E - 1, TILES - 1]))
            then(dve.tensor_tensor(count, run[:, :, TILES - 1], starts, ALU.subtract))
            then(dve.tensor_scalar(counti.bitcast(I32), count, float(P - 1), None, ALU.add))
            then(dve.tensor_scalar(counti.bitcast(I32), counti.bitcast(I32), 7, None, ALU.logical_shift_right))
            then(dve.tensor_copy(ntile, counti.bitcast(I32)))
            then(dve.tensor_tensor_scan(tbend, ones_r[:, 0:E], ntile, 0.0, ALU.mult, ALU.add))
            then(dve.tensor_tensor(adj, tbend, ntile, ALU.subtract))
            then(dve.scalar_tensor_tensor(adj, adj, float(P), starts, ALU.mult, ALU.subtract))
            then(dve.tensor_tensor(run, run, tot, ALU.subtract))
            then(dve.tensor_tensor(run, run, adj.rearrange("p (e t) -> p e t", t=1).to_broadcast([P, E, TILES]), ALU.add))
            then(dve.tensor_tensor(slots, pv[:, 0:P].rearrange("p (t e) -> p t e", e=E),
                                   run.rearrange("p e t -> p t e"), ALU.add))
            for c in range(TOPK):
                then(dve.tensor_tensor(picked, slots, hot[c], ALU.mult))
                then(dve.tensor_reduce(slotf[:, c], picked, AX.X, ALU.add))
            then(dve.tensor_copy(sloti.bitcast(I32), slotf.rearrange("p c t -> p (c t)")))
            dve.tensor_scalar(tilei.bitcast(I32), sloti.bitcast(I32), 7, None, ALU.logical_shift_right)
            then(dve.tensor_scalar(posi.bitcast(I32), sloti.bitcast(I32), P - 1, None, ALU.bitwise_and))
            dve.tensor_copy(tile_n, tilei.bitcast(I32))
            then(dve.tensor_copy(pos_n, posi.bitcast(I32)))
            dve.wait_ge(ex_ready, 1)
            then(dve.tensor_scalar(den, ex, 1.0, None, ALU.add))
            then(dve.reciprocal(weight[:, 0, :], den))
            then(dve.tensor_tensor(weight[:, 1, :], weight[:, 0, :], ex, ALU.mult))
            both_w = weight[:, :, :].rearrange("p c t -> p (c t)")
            dve.tensor_copy(token1h, token1[:, 0:TILES])
            then(dve.tensor_copy(w_hi, both_w))
            then(dve.tensor_tensor(w_rest, both_w, w_hi, ALU.subtract))
            dve.tensor_scalar(w_lo, w_rest, float(LOW), None, ALU.mult)
            then(dve.tensor_tensor(at_tile, tau[:, :, 0].rearrange("p (i t) -> p i t", i=1).to_broadcast([P, PAIRS, XS_TILES]),
                                   tile_n.rearrange("p (i t) -> p i t", t=1).to_broadcast([P, PAIRS, XS_TILES]), ALU.is_equal))
            for c in range(TOPK):
                pairs = slice(c * TILES, (c + 1) * TILES)
                dve.tensor_tensor(marks[:, 0, pairs], at_tile[:, pairs],
                                  token1h.rearrange("p (i t) -> p i t", t=1).to_broadcast([P, TILES, XS_TILES]), ALU.mult)
            for m, part in ((1, w_hi), (2, w_lo)):
                last = dve.tensor_tensor(marks[:, m], at_tile,
                                         part.rearrange("p (i t) -> p i t", t=1).to_broadcast([P, PAIRS, XS_TILES]), ALU.mult)
            then(last)
            for i in range(PAIRS):
                if i >= 4:
                    dve.wait_ge(pos_mm, i - 3)
                dve.tensor_scalar(at_pos[:, i % 4, :], cols, pos_n[:, i:i + 1], None, ALU.is_equal).then_inc(pos_ready, 1)
            then(dve.tensor_tensor(tge, tau, tbend.rearrange("p (t e) -> p t e", t=1).to_broadcast([P, XS_TILES, E]),
                                   ALU.is_ge))
            then(dve.tensor_reduce(tilef, tge, AX.X, ALU.add))
            dve.tensor_scalar(expert_of[:, :], tilef, float(E - 1), None, ALU.min).then_inc(table_ready, 1)
            dve.wait_ge(pos_mm, PAIRS)
            found = pc[:, 0, 0:XS_TILES]
            dve.tensor_scalar(empty, found, 0.5, token1[:, TILES:TILES + 1], ALU.is_lt, ALU.mult)
            then(dve.tensor_scalar(loadf, found, -1.0, 0.0, ALU.add, ALU.max))
            then(dve.tensor_copy(weight_of[:, :], pc[:, 0, XS_TILES:2 * XS_TILES]))
            dve.scalar_tensor_tensor(weight_of[:, :], pc[:, 0, 2 * XS_TILES:3 * XS_TILES], 1.0 / LOW, weight_of[:, :], ALU.mult,
                                     ALU.add).then_inc(table_ready, 1)
            dve.tensor_copy(token_of[:, :], loadf).then_inc(table_ready, 1)
            then(dve.scalar_tensor_tensor(empty, found, -1.0, empty, ALU.add, ALU.add))
            dve.tensor_copy(sum_of[:, :], empty).then_inc(table_ready, 1)
            dve.wait_ge(table_ready, TABLES)
            assert steps[0] == ROUTE_STEPS

            dve.wait_ge(late_in, 2 * 16)

            def hidden(t, e):
                for n in range(2):
                    dve.wait_ge(h_mm, t * 2 + n + 1)
                    dve.tensor_tensor(hb[:, n * 512:(n + 1) * 512], pa[:, n, :],
                                      b1_s[:, bass.ds(e, 1), n * 512:(n + 1) * 512].rearrange("p a f -> p (a f)"),
                                      ALU.add).then_inc(hb_ready, 1)

            def copy_hgT(t):
                dve.wait_ge(hgT_mm, t * 2 + 2)
                dve.tensor_copy(hgT[:, KF // 2:KF, :],
                                pb[:, 1, :].rearrange("p (k q) -> p k q", k=KF // 2)).then_inc(hgT_ready, 1)

            def finish_tile(n, e):
                dve.wait_ge(y_mm, n)
                dve.tensor_tensor(yt, pv[:, 0:D], b2_s[:, bass.ds(e, 1), :].rearrange("p a d -> p (a d)"),
                                  ALU.add).then_inc(yb_ready, 1)
                dve.wait_ge(yb_ready, n)
                dve.tensor_scalar(yt, yt, weight_of[:, bass.ds(n - 1, 1)], None, ALU.mult).then_inc(y_ready, 1)

            def expert(t):
                return nc.values_load(expert_of[0:1, bass.ds(t, 1)], engines=[mybir.EngineType.DVE], min_val=0, max_val=E - 1,
                                      skip_runtime_bounds_check_because="the table is clamped to the experts")

            hidden(0, expert(0))
            copy_hgT(0)
            dve.wait_ge(b2_in, 16)
            with dve.Fori(1, SLOT_TILES) as t:
                hidden(t, expert(t))
                finish_tile(t, expert(t - 1))
                copy_hgT(t)
                dve.wait_ge(y_out, t * 16)
            finish_tile(SLOT_TILES, expert(SLOT_TILES - 1))

            dve.wait_ge(ln_in, 2 * 16)

            def sum_moments(g):
                dve.wait_ge(sum_in[g], 16)
                moments(OUT_NORMS[g % 2], total[:, g * CT:(g + 1) * CT, :], EPS_FFN, CHUNKS + g // 2 + 1)

            def scale_and_add(g):
                norm = OUT_NORMS[g % 2]
                dve.wait_ge(norm["rstd_ready"], CHUNKS + g // 2 + 1)
                for j in range(CT):
                    last = dve.scalar_tensor_tensor(zed[:, j, :], total[:, g * CT + j, :], norm["mean"][:, j:j + 1], lnw_s,
                                                    ALU.subtract, ALU.mult)
                last.then_inc(fin_step, 1)
                dve.wait_ge(fin_step, 2 * g + 1)
                dve.wait_ge(base_ready, g + 1)
                for j in range(CT):
                    last = dve.scalar_tensor_tensor(fin[:, g * CT + j, :], zed[:, j, :], norm["rstd"][:, j:j + 1],
                                                    fin[:, g * CT + j, :], ALU.mult, ALU.add)
                last.then_inc(fin_step, 1)
                dve.wait_ge(fin_step, 2 * g + 2)
                if g >= 1:
                    dve.wait_ge(fin_ready, g)
                moments(LN2, fin[:, g * CT:(g + 1) * CT, :], EPS, CHUNKS + g + 1)
                dve.tensor_scalar(neg_mean[:, :], LN2["msum"][:, :], -0.5, None, ALU.mult).then_inc(neg_mean_ready, 1)

            sum_moments(0)
            for g in range(GROUPS):
                if g + 1 < GROUPS:
                    sum_moments(g + 1)
                scale_and_add(g)

        @block.tensor
        def _(pe):
            def context():
                pe.wait_ge(ctx_in, 8 * 16)
                for c in range(KD):
                    for k in range(KD):
                        pe.matmul(pa[:, c, 0:B * SC], wxk_s[:, k, c * P:(c + 1) * P], ctx_s[:, k, :], start=(k == 0),
                                  stop=(k == KD - 1))
                for b in range(B):
                    for k in range(KD):
                        last = pe.matmul(pc[0:SC, b, 0:D], ctx_s[:, k, b * SC:(b + 1) * SC], wxv_s[:, k, :], start=(k == 0),
                                         stop=(k == KD - 1))
                last.then_inc(ctx_mm, 1)

            pe.wait_ge(made, MADE)

            def project(dst, w, src, halves=range(KD)):
                for c in halves:
                    for k in range(KD):
                        last = pe.matmul(dst[:, c, :], w[:, k, c * P:(c + 1) * P], src[:, k, :], start=(k == 0),
                                         stop=(k == KD - 1))
                return last

            def to_features(dst, src):
                for j in range(CT):
                    for k in range(KD):
                        last = pe.transpose(dst[:, k, j * P:(j + 1) * P], src[:, j, k * P:(k + 1) * P], ident[:, :])
                return last

            def normalised(n):
                pe.wait_ge(h0_ready, n + 1)
                to_features(pb, h0).then_inc(hT_mm, 1)

            def keys(n):
                pe.wait_ge(hT_ready, n + 1)
                project(pb, wk_s, hT).then_inc(k_mm, 1)

            def key_weights(n):
                pe.wait_ge(kT_ready, n + 1)
                project(pb, wka_s, keysT).then_inc(ka_mm, 1)

            def values(n, half, prev=None):
                if half == 0:
                    pe.wait_ge(kexp_ready, n + 1)
                    if prev is not None:
                        pe.wait_ge(lg_ready, prev + 1)
                project(pb, wv_s, hT, [half]).then_inc(v_mm, 1)

            def turn_attention(n):
                pe.wait_ge(attn_ready, n + 1)
                for j in range(CT):
                    for k in range(KD):
                        last = pe.transpose(pb_t[:, j, k * P:(k + 1) * P], attnT[:, k, j * P:(j + 1) * P], ident[:, :])
                last.then_inc(at_mm, 1)

            def x1_features(n):
                pe.wait_ge(x1_ready, n + 1)
                to_features(pb, x1).then_inc(x1T_mm, 1)

            def queries(n):
                pe.wait_ge(x1T_ready, n + 1)
                project(pb, wq_s, x1T).then_inc(q_mm, 1)

            def output_features(it):
                pe.wait_ge(x2_ready, it + 1)
                to_features(pb, x2c).then_inc(x2T_mm, 1)

            def route_logits(it):
                pe.wait_ge(x2T_ready, it + 1)
                for j in range(CT):
                    for k in range(KD):
                        last = pe.matmul(pb[:, 0, j * E:(j + 1) * E], x2T[:, k, j * P:(j + 1) * P], rw_s[:, k, :],
                                         start=(k == 0), stop=(k == KD - 1))
                last.then_inc(lg_mm, 1)

            def cross_attention(it, nxt, prev):
                b = it // CPB

                def scores(h):
                    j, quad = divmod(h, QUADS)
                    half, g = divmod(quad, HC // HG)
                    if h >= 2:
                        pe.wait_ge(sub_ready, it * STEPS + h - 1)
                    dst = pa[:, h % 2, 0:HG * SC]
                    pe.matmul(dst, qT[:, half, j * P:(j + 1) * P],
                              kbd[:, bass.ds(b, 1), half, g * HG:(g + 1) * HG, :].rearrange("p a h k -> p (a h k)"),
                              start=True, stop=False)
                    pe.matmul(dst, mask_b[0:SC, bass.ds((it % CPB) * CHUNK + j * P, P)],
                              eye4[0:SC, :, :].rearrange("p h k -> p (h k)"), start=False, stop=True).then_inc(s_mm, 1)

                def turn_probs(h):
                    pe.wait_ge(exp_ready, it * STEPS + h + 1)
                    if h >= 2:
                        pe.wait_ge(pT_ready, it * STEPS + h - 1)
                    for n in range(HG):
                        last = pe.transpose(pc[0:SC, h % 2, n * P:(n + 1) * P], prob[:, h % RING, n, :], ident[:, :])
                    last.then_inc(pT_mm, 1)

                def weigh_values(h):
                    j, quad = divmod(h, QUADS)
                    pe.wait_ge(pT_ready, it * STEPS + h + 1)
                    if quad == 0 and j >= 1:
                        pe.wait_ge(merged_ready, it * CT + j)
                    for n in range(HG):
                        head = quad * HG + n
                        last = pe.matmul(pv[:, head * VW:(head + 1) * VW], probT[0:SC, h % RING, n, :],
                                         vaug[0:SC, bass.ds(b, 1), head, :].rearrange("p a v -> p (a v)"),
                                         start=True, stop=True)
                    if quad == QUADS - 1:
                        last.then_inc(pv_mm, 1)

                def turn_heads(j):
                    pe.wait_ge(merged_ready, it * CT + j + 1)
                    for k in range(KD):
                        last = pe.transpose(pm[:, k * P:(k + 1) * P], merged[:, j % 2, k * P:(k + 1) * P], ident[:, :])
                    last.then_inc(mT_mm, 1)

                def project_out(j):
                    pe.wait_ge(mT_ready, it * CT + j + 1)
                    if j >= 1:
                        pe.wait_ge(r2_ready, it * CT + j)
                    for k in range(KD):
                        last = pe.matmul(pm[:, D:2 * D], mergedT[:, j % 2, k, :], wo_s[:, k, :], start=(k == 0),
                                         stop=(k == KD - 1))
                    last.then_inc(o_mm, 1)

                pe.wait_ge(qT_ready, it + 1)
                scores(0)
                scores(1)
                turn_probs(0)
                for h in range(STEPS):
                    if h + 2 < STEPS:
                        scores(h + 2)
                    if h + 1 < STEPS:
                        turn_probs(h + 1)
                    weigh_values(h)
                    if h >= QUADS and h % QUADS == 0:
                        turn_heads(h // QUADS - 1)
                    if h >= QUADS and h % QUADS == 1:
                        project_out(h // QUADS - 1)
                    if nxt is not None:
                        if h == 1:
                            normalised(nxt)
                        if h == 2:
                            keys(nxt)
                        if h == 3:
                            key_weights(nxt)
                    if prev is not None:
                        if h == 5:
                            output_features(prev)
                        if h == 6:
                            route_logits(prev)
                    if nxt is not None:
                        if h == 8:
                            values(nxt, 0, prev)
                        if h == 9:
                            values(nxt, 1, prev)
                        if h == 11:
                            turn_attention(nxt)
                        if h == 13:
                            x1_features(nxt)
                turn_heads(CT - 1)
                if nxt is not None:
                    queries(nxt)
                project_out(CT - 1)

            normalised(0)
            pe.wait_ge(weights_in, 3 * 16)
            keys(0)
            key_weights(0)
            context()
            for half in range(KD):
                values(0, half)
            turn_attention(0)
            x1_features(0)
            pe.wait_ge(kv_made, 1)
            queries(0)
            cross_attention(0, 1, None)
            with pe.Fori(1, CHUNKS - 1) as it:
                cross_attention(it, it + 1, it - 1)
            cross_attention(CHUNKS - 1, None, CHUNKS - 2)
            output_features(CHUNKS - 1)
            route_logits(CHUNKS - 1)

            pe.wait_ge(route_consts, 7)
            pe.wait_ge(route, ROUTE_BOTH)
            chosen = both.rearrange("p t e -> p (t e)")
            pe.matmul(pv[:, 0:P], tri, chosen, start=True, stop=True)
            pe.matmul(pv[:, P:2 * P], ones_m, chosen, start=True, stop=True).then_inc(count_mm, 1)
            for i in range(PAIRS):
                pe.wait_ge(pos_ready, i + 1)
                pe.matmul(pc[:, 0, 0:3 * XS_TILES].rearrange("p (m t) -> p m t", m=3), at_pos[:, i % 4, :], marks[:, :, i, :], start=(i == 0),
                          stop=(i == PAIRS - 1)).then_inc(pos_mm, 1)

            def expert(t):
                return nc.values_load(expert_of[0:1, bass.ds(t, 1)], engines=[mybir.EngineType.PE], min_val=0, max_val=E - 1,
                                      skip_runtime_bounds_check_because="the table is clamped to the experts")

            def turn_rows(n):
                pe.wait_ge(xt_in, n * 16)
                for k in range(KD):
                    last = pe.transpose(pm[:, k * P:(k + 1) * P], xt[:, k * P:(k + 1) * P], ident[:, :])
                last.then_inc(xt_mm, 1)

            def up(t, e):
                pe.wait_ge(xt_ready, t + 1)
                for n in range(2):
                    for k in range(KD):
                        last = pe.matmul(pa[:, n, :], xtT[:, k, :],
                                         w1_v[:, bass.ds(e, 1), k, n * 512:(n + 1) * 512].rearrange("p a f -> p (a f)"),
                                         start=(k == 0), stop=(k == KD - 1))
                    last.then_inc(h_mm, 1)

            def down(n, e):
                pe.wait_ge(hgT_ready, n * 2)
                for k in range(KF):
                    last = pe.matmul(pv[:, 0:D], hgT[:, k, :], w2_v[:, bass.ds(e, 1), k, :].rearrange("p a d -> p (a d)"),
                                     start=(k == 0), stop=(k == KF - 1))
                last.then_inc(y_mm, 1)

            def turn_hidden(t):
                for n in range(2):
                    pe.wait_ge(hg_ready, t * 2 + n + 1)
                    for k in range(KF // 2):
                        q = n * (KF // 2) + k
                        last = pe.transpose(pb[:, n, k * P:(k + 1) * P], hg[:, q * P:(q + 1) * P], ident[:, :])
                    last.then_inc(hgT_mm, 1)

            pe.wait_ge(table_ready, 1)
            turn_rows(1)
            pe.wait_ge(experts_in, 2 * E * 16)
            up(0, expert(0))
            turn_rows(2)
            turn_hidden(0)
            with pe.Fori(1, SLOT_TILES) as t:
                up(t, expert(t))
                down(t, expert(t - 1))
                turn_rows(t + 2)
                turn_hidden(t)
            down(SLOT_TILES, expert(SLOT_TILES - 1))


MADE = 9
ROUTE_BOTH = 12
ROUTE_DIFF = 13
ROUTE_STEPS = ROUTE_DIFF + 14 + 2 * TOPK + 3 + 2 + 5 + 2 + 3
TABLES = 4


def kernel(**inputs):
    import numpy as np
    import concourse.bacc as bacc
    from concourse.bass_utils import run_bass_kernel_spmd

    def a(name, pre="L0_"):
        return np.asarray(inputs[pre + name])

    def turned(w, *axes):
        return np.ascontiguousarray(w.transpose(*axes)) if axes else np.ascontiguousarray(w.T)

    mask = a("mask_1x1xSxS2_bk1", "").reshape(S, SC)
    arrays = {
        "x": np.ascontiguousarray(a("x", "").reshape(T, D)),
        "ctxT": turned(a("ctx_1024", "").reshape(B * SC, D)),
        "maskT": turned(mask),
        "wk": turned(a("attn_Wk")), "bk": a("attn_bk"), "wka": turned(a("attn_Wka")), "bka": a("attn_bka"),
        "wv": turned(a("attn_Wv")), "bv": a("attn_bv"), "gamma": a("attn_gamma"), "beta": a("attn_beta"),
        "wq": turned(a("xattn_W_q")), "wxk": turned(a("xattn_W_k")), "wxv": turned(a("xattn_W_v")), "wo": turned(a("xattn_W_o")),
        "rw": turned(a("ffn_router_w")), "rb": a("ffn_router_b"),
        "w1": turned(a("ffn_w1"), 0, 2, 1), "b1": a("ffn_b1"), "w2": turned(a("ffn_w2"), 0, 2, 1), "b2": a("ffn_b2"),
        "lnw": a("ffn_ln_w"), "lnb": a("ffn_ln_b"),
    }
    nc = bacc.Bacc("TRN2", target_bir_lowering=False, num_devices=1)
    args = {n: nc.dram_tensor(f"in_{n}", v.shape, mybir.dt.from_np(v.dtype), kind="ExternalInput").ap()
            for n, v in arrays.items()}
    result = nc.dram_tensor("out", (T, D), F32, kind="ExternalOutput").ap()
    decoder_layer(nc, out=result, **args)
    r = run_bass_kernel_spmd(nc, [{f"in_{n}": v for n, v in arrays.items()}], core_ids=[0])
    return np.asarray(r.results[0]["out"]).reshape(B, S, D)
```
